# Optimizing a Trainium2 kernel written in Bass

```python
import numpy as np
import jax
import jax.numpy as jnp

def _softmax(x, axis=-1):
    return jax.nn.softmax(x, axis=axis)

def _gelu(x):
    return jax.nn.gelu(x, approximate=True)

def _silu(x):
    return jax.nn.silu(x)

def _sigmoid(x):
    return jax.nn.sigmoid(x)

def _layernorm(x, axis=-1, eps=1e-05):
    m = jnp.mean(x, axis=axis, keepdims=True)
    v = jnp.var(x, axis=axis, keepdims=True)
    return (x - m) / jnp.sqrt(v + eps)

def _scatter_add(tgt, idx, src, axis=0):
    return tgt.at[idx].add(src)

def _segment_sum(src, seg, n):
    return jax.ops.segment_sum(src, seg, n)
kernel_name = 'mk_seq_postln_d1_jaxref_r8_30e129'

def setup_inputs(seed: int=0):
    np.random.seed(seed)
    _w = jnp.asarray

    def _L0_attn_setup():
        import jax, jax.numpy as jnp
        import numpy as np
        DIM = 128
        key = jax.random.key(seed)
        k1, k2, k3, k4, k5 = jax.random.split(key, 5)
        x = jax.random.normal(k1, (4, 256, DIM), dtype=jnp.float32)
        w_qkv = jax.random.normal(k2, (DIM, 3 * DIM), dtype=jnp.float32) * DIM ** (-0.5)
        b_qkv = jax.random.normal(k3, (3 * DIM,), dtype=jnp.float32) * 0.02
        w_proj = jax.random.normal(k4, (DIM, DIM), dtype=jnp.float32) * DIM ** (-0.5)
        b_proj = jax.random.normal(k5, (DIM,), dtype=jnp.float32) * 0.02
        return {'x': x, 'w_qkv': w_qkv, 'b_qkv': b_qkv, 'w_proj': w_proj, 'b_proj': b_proj}
    _L0_attn_in = _L0_attn_setup()

    def _L0_ffn_setup():
        import math
        import jax, jax.numpy as jnp
        import numpy as np
        HIDDEN = 128
        INTER = 512
        EXPERTS = 8
        B, T = (4, 256)
        EPS = 1e-12
        CAP_FACTOR = 1.0
        MIN_CAP = 4

        def layer_norm(x, g, b, eps=EPS):
            m = jnp.mean(x, axis=-1, keepdims=True)
            v = jnp.var(x, axis=-1, keepdims=True)
            return (x - m) * jax.lax.rsqrt(v + eps) * g + b

        def top1_gate(x, wg, capacity):
            logits = x @ wg
            gates = jax.nn.softmax(logits, axis=-1)
            E = wg.shape[-1]
            idx = jnp.argmax(gates, axis=-1)
            mask1 = jax.nn.one_hot(idx, E, dtype=gates.dtype)
            locations = jnp.cumsum(mask1, axis=0) - mask1
            mask1 = mask1 * (locations < capacity).astype(gates.dtype)
            gates1_s = jnp.sum(gates * mask1, axis=-1)
            loc_s = jnp.sum(locations * mask1, axis=-1).astype(jnp.int32)
            loc_oh = jax.nn.one_hot(loc_s, capacity, dtype=gates.dtype)
            combine = gates1_s[:, None, None] * mask1[:, :, None] * loc_oh[:, None, :]
            dispatch = jax.lax.stop_gradient((combine > 0).astype(x.dtype))
            return (combine, dispatch)
        key = jax.random.key(seed)
        ks = jax.random.split(key, 8)
        s = 0.02
        return {'x': jax.random.normal(ks[0], (B, T, HIDDEN), jnp.float32), 'attn_nw': jnp.ones((HIDDEN,), jnp.float32), 'attn_nb': jnp.zeros((HIDDEN,), jnp.float32), 'wg': jax.random.normal(ks[1], (HIDDEN, EXPERTS), jnp.float32) * s, 'inter_w': jax.random.normal(ks[2], (EXPERTS, HIDDEN, INTER), jnp.float32) * s, 'inter_b': jnp.zeros((EXPERTS, INTER), jnp.float32), 'output_w': jax.random.normal(ks[3], (EXPERTS, INTER, HIDDEN), jnp.float32) * s, 'output_b': jnp.zeros((EXPERTS, HIDDEN), jnp.float32), 'res_inter_w': jax.random.normal(ks[4], (HIDDEN, INTER), jnp.float32) * s, 'res_inter_b': jnp.zeros((INTER,), jnp.float32), 'res_output_w': jax.random.normal(ks[5], (INTER, HIDDEN), jnp.float32) * s, 'res_output_b': jnp.zeros((HIDDEN,), jnp.float32), 'res_coef': jax.random.normal(ks[6], (HIDDEN, 2), jnp.float32) * s}
    _L0_ffn_in = _L0_ffn_setup()
    _d = {'L0_attn_x': _L0_attn_in['x'], 'L0_attn_w_qkv': _L0_attn_in['w_qkv'], 'L0_attn_b_qkv': _L0_attn_in['b_qkv'], 'L0_attn_w_proj': _L0_attn_in['w_proj'], 'L0_attn_b_proj': _L0_attn_in['b_proj'], 'L0_ffn_attn_nw': _L0_ffn_in['attn_nw'], 'L0_ffn_attn_nb': _L0_ffn_in['attn_nb'], 'L0_ffn_wg': _L0_ffn_in['wg'], 'L0_ffn_inter_w': _L0_ffn_in['inter_w'], 'L0_ffn_inter_b': _L0_ffn_in['inter_b'], 'L0_ffn_output_w': _L0_ffn_in['output_w'], 'L0_ffn_output_b': _L0_ffn_in['output_b'], 'L0_ffn_res_inter_w': _L0_ffn_in['res_inter_w'], 'L0_ffn_res_inter_b': _L0_ffn_in['res_inter_b'], 'L0_ffn_res_output_w': _L0_ffn_in['res_output_w'], 'L0_ffn_res_output_b': _L0_ffn_in['res_output_b'], 'L0_ffn_res_coef': _L0_ffn_in['res_coef']}
    _x0 = _d['L0_attn_x']
    _d['L0_attn_x'] = jax.random.normal(jax.random.fold_in(jax.random.key(seed), 1), (16, 512, 128), dtype=_x0.dtype)
    del _x0
    return _d

def reference(L0_attn_x, L0_attn_w_qkv, L0_attn_b_qkv, L0_attn_w_proj, L0_attn_b_proj, L0_ffn_attn_nw, L0_ffn_attn_nb, L0_ffn_wg, L0_ffn_inter_w, L0_ffn_inter_b, L0_ffn_output_w, L0_ffn_output_b, L0_ffn_res_inter_w, L0_ffn_res_inter_b, L0_ffn_res_output_w, L0_ffn_res_output_b, L0_ffn_res_coef):

    def _L0_attn_ref(x, w_qkv, b_qkv, w_proj, b_proj):
        import jax, jax.numpy as jnp
        import numpy as np
        DIM = 128
        qkv = jnp.einsum('bsd,de->bse', x, w_qkv) + b_qkv
        q, k, v = jnp.split(qkv, 3, axis=-1)
        scale = jnp.asarray(DIM ** 0.5, dtype=x.dtype)
        attn = jnp.einsum('bqd,bkd->bqk', q, k) / scale
        attn = jax.nn.softmax(attn, axis=-1)
        out = jnp.einsum('bqk,bkd->bqd', attn, v)
        return jnp.einsum('bsd,de->bse', out, w_proj) + b_proj

    def _L0_ffn_ref(x, attn_nw, attn_nb, wg, inter_w, inter_b, output_w, output_b, res_inter_w, res_inter_b, res_output_w, res_output_b, res_coef):
        import math
        import jax, jax.numpy as jnp
        import numpy as np
        HIDDEN = 128
        INTER = 512
        EXPERTS = 8
        B, T = (4, 256)
        EPS = 1e-12
        CAP_FACTOR = 1.0
        MIN_CAP = 4

        def layer_norm(x, g, b, eps=EPS):
            m = jnp.mean(x, axis=-1, keepdims=True)
            v = jnp.var(x, axis=-1, keepdims=True)
            return (x - m) * jax.lax.rsqrt(v + eps) * g + b

        def top1_gate(x, wg, capacity):
            logits = x @ wg
            gates = jax.nn.softmax(logits, axis=-1)
            E = wg.shape[-1]
            idx = jnp.argmax(gates, axis=-1)
            mask1 = jax.nn.one_hot(idx, E, dtype=gates.dtype)
            locations = jnp.cumsum(mask1, axis=0) - mask1
            mask1 = mask1 * (locations < capacity).astype(gates.dtype)
            gates1_s = jnp.sum(gates * mask1, axis=-1)
            loc_s = jnp.sum(locations * mask1, axis=-1).astype(jnp.int32)
            loc_oh = jax.nn.one_hot(loc_s, capacity, dtype=gates.dtype)
            combine = gates1_s[:, None, None] * mask1[:, :, None] * loc_oh[:, None, :]
            dispatch = jax.lax.stop_gradient((combine > 0).astype(x.dtype))
            return (combine, dispatch)
        Bx, Tx, M = x.shape
        S = Bx * Tx
        E = wg.shape[-1]
        capacity = max(MIN_CAP, math.ceil(S / E * CAP_FACTOR))
        residual = x.reshape(S, M)
        attn_out = layer_norm(residual, attn_nw, attn_nb)
        combine, dispatch = top1_gate(attn_out, wg, capacity)
        dispatched = jnp.einsum('sec,sm->ecm', dispatch, attn_out)
        h = jax.nn.gelu(jnp.einsum('ecm,emi->eci', dispatched, inter_w) + inter_b[:, None, :], approximate=True)
        expert_out = jnp.einsum('eci,eim->ecm', h, output_w) + output_b[:, None, :]
        moe_out = jnp.einsum('sec,ecm->sm', combine, expert_out)
        rh = jax.nn.gelu(attn_out @ res_inter_w + res_inter_b, approximate=True)
        res_mlp_out = rh @ res_output_w + res_output_b
        coef = jax.nn.softmax(attn_out @ res_coef, axis=-1)
        out = res_mlp_out * coef[:, :1] + moe_out * coef[:, 1:]
        out = out + residual
        return out.reshape(Bx, Tx, M)
    x = L0_attn_x
    x = _layernorm(x + _L0_attn_ref(x, L0_attn_w_qkv, L0_attn_b_qkv, L0_attn_w_proj, L0_attn_b_proj), axis=-1)
    x = _layernorm(x + _L0_ffn_ref(x, L0_ffn_attn_nw, L0_ffn_attn_nb, L0_ffn_wg, L0_ffn_inter_w, L0_ffn_inter_b, L0_ffn_output_w, L0_ffn_output_b, L0_ffn_res_inter_w, L0_ffn_res_inter_b, L0_ffn_res_output_w, L0_ffn_res_output_b, L0_ffn_res_coef), axis=-1)
    return x

_drawn_inputs = setup_inputs


def setup_inputs(seed=0):
    import zlib

    import numpy as np

    out = dict(_drawn_inputs(seed))
    spreads = {'L0_ffn_attn_nw': (1.0, 0.6),
     'L0_ffn_attn_nb': (0.0, 0.8),
     'L0_ffn_inter_b': (0.0, 0.8),
     'L0_ffn_output_b': (0.0, 0.8),
     'L0_ffn_res_inter_b': (0.0, 0.8),
     'L0_ffn_res_output_b': (0.0, 0.313)}
    factors = {'L0_attn_b_qkv': 2.675,
     'L0_attn_b_proj': 2.765,
     'L0_ffn_wg': 8.0,
     'L0_ffn_inter_w': 8.0,
     'L0_ffn_output_w': 8.0,
     'L0_ffn_res_inter_w': 4.013,
     'L0_ffn_res_output_w': 3.723,
     'L0_ffn_res_coef': 8.0}
    for name, (base, spread) in spreads.items():
        noise = np.random.default_rng([zlib.crc32(name.encode()), seed]).standard_normal(out[name].shape)
        drawn = base * np.exp(spread * noise) if base else spread * noise
        out[name] = jnp.asarray(drawn.astype(out[name].dtype))
    for name, factor in factors.items():
        out[name] = (out[name] * factor).astype(out[name].dtype)
    return out
```

```python
from contextlib import ExitStack

import concourse.bass as bass
from concourse import mybir

F32 = mybir.dt.float32
F32R = mybir.dt.float32r
BF16 = mybir.dt.bfloat16
U32 = mybir.dt.uint32
ALU = mybir.AluOpType
ACT = mybir.ActivationFunctionType
AX = mybir.AxisListType

P = 128
LN_EPS = 1e-5
GATE_LN_EPS = 1e-12


def build(nc, x_tok, x_T, wqT, wkT, wvT, w_proj, b_q, b_v, b_proj, ln_w, ln_b, w_gate, w_coef, inter_w, inter_bT,
          output_w, output_bT, res_w, res_bT, res_out_w, res_out_bT, consts, out):
    NB, T, D = x_tok.shape
    J = T // P
    E, _, I = inter_w.shape
    IC = I // P
    S = NB * T
    CAP = max(4, -(-S // E))
    TPE = CAP // T
    NG = E + 2
    assert D == P and J == 4 and TPE == 2 and NB % 2 == 0

    slots_dram = nc.dram_tensor("slots_dram", [S, D], F32).ap()
    moe_dram = nc.dram_tensor("moe_dram", [S + 1, D], F32).ap()

    MS = 5

    def moments(ve, stats, mom, mean, var, steps, done, mean_free):
        ve.tensor_reduce(mom[:, :, 0:2], stats[:].rearrange("p j (h f) -> p j f h", h=2)[:, :, 1:3], AX.X, ALU.add)\
            .then_inc(steps, 1)
        ve.tensor_tensor(mom[:, :, 2], stats[:, :, 1], stats[:, :, 4], ALU.subtract).then_inc(steps, 1)
        ve.wait_ge(steps, done + 2)
        ve.scalar_tensor_tensor(var[:], mom[:, :, 2], 0.25, mom[:, :, 2], ALU.mult, ALU.mult).then_inc(steps, 1)
        mean_free()
        ve.tensor_scalar(mean, mom[:, :, 0], 0.5, None, ALU.mult).then_inc(steps, 1)
        ve.wait_ge(steps, done + 3)
        ve.scalar_tensor_tensor(var[:], mom[:, :, 1], 1.0 / D, var[:], ALU.mult, ALU.add).then_inc(steps, 1)

    with ExitStack() as ctx:
        def sb(name, shape, dt=F32):
            return ctx.enter_context(nc.sbuf_tensor(name, shape, dt))

        def sem(name):
            return ctx.enter_context(nc.semaphore(name))

        w_raw = sb("w_raw", [P, 4, D])
        vecs = sb("vecs", [P, 4])
        bproj_row = sb("bproj_row", [1, D])
        gc_raw = sb("gc_raw", [P, NG])
        gc_w = sb("gc_w", [P, NG])
        gc_bias = sb("gc_bias", [P, NG])
        cst = sb("cst", [P, 2 * P + J * E])
        ident_b = sb("ident_b", [P, P], BF16)
        upper_b = sb("upper_b", [P, P], BF16)
        ones_b = sb("ones_b", [P, P], BF16)
        ones_row = sb("ones_row", [1, P])
        bv_b = sb("bv_b", [P, P])
        lnb_b = sb("lnb_b", [P, P])
        expo = sb("expo", [P, 2 * J])
        a_f = sb("a_f", [P, D])
        aH = sb("aH", [P, D], F32R)
        aL = sb("aL", [P, D], F32R)
        c_z = sb("c_z", [P, 1])
        w_vp = sb("w_vp", [P, D])
        b_vp = sb("b_vp", [P, D])
        zero_t = sb("zero_t", [P, 2048])
        res_raw = sb("res_raw", [P, I])
        res_s = sb("res_s", [P, I])
        resH = sb("resH", [P, I], F32R)
        resL = sb("resL", [P, I], F32R)
        res_bias = sb("res_bias", [P, IC])
        res_bcol = sb("res_bcol", [P, IC])
        res_out = sb("res_out", [P, IC, D])
        res_obcol = sb("res_obcol", [P, 1])
        e_bcol = sb("e_bcol", [P, E, IC])
        e_obcol = sb("e_obcol", [P, E])
        ident = cst[:, 0:P]
        desc = cst[:, 2 * P:2 * P + J * E].rearrange("p (j e) -> p j e", j=J)

        xn_all = sb("xn_all", [P, NB, J * D])
        xnH_all = sb("xnH_all", [P, NB, T], F32R)
        xnL_all = sb("xnL_all", [P, NB, T], F32R)
        slot_all = sb("slot_all", [P, NB, J], U32)
        coef_all = sb("coef_all", [P, NB, 3 * J])

        psum = [ctx.enter_context(nc.psum_tensor(f"bank{i}", [P, 512], F32)) for i in range(8)]

        with ExitStack() as c1:
            def sb1(name, shape, dt=F32):
                return c1.enter_context(nc.sbuf_tensor(name, shape, dt))

            def sem1(name):
                return c1.enter_context(nc.semaphore(name))

            xt_in = sb1("xt_in", [P, 2, T])
            x_in = sb1("x_in", [P, 2, J, D])
            xtH = sb1("xtH", [P, 2, T], F32R)
            xtL = sb1("xtL", [P, 2, T], F32R)
            xb = sb1("xb", [P, 2, J, D])
            zH = sb1("zH", [P, 2, T], F32R)
            zL = sb1("zL", [P, 2, T], F32R)
            nmax = sb1("nmax", [P, 2, J])
            rsum = sb1("rsum", [P, 2, J])
            rinv = sb1("rinv", [P, J])
            prob = sb1("prob", [P, J, T])
            probT = sb1("probT", [P, 2, J, T])
            oT = sb1("oT", [P, T])
            r1 = sb1("r1", [P, 2, J, D])
            stats = sb1("stats", [P, J, 6])
            mom = sb1("mom", [P, J, 3])
            mean = sb1("mean", [P, 2, J])
            var = sb1("var", [P, J])
            vq = sb1("vq", [P, 2, 3, J])
            rs = sb1("rs", [P, 2, 2, J])
            srt = sb1("srt", [P, J])
            xn = sb1("xn", [P, 2, J, D])
            xnT_f = sb1("xnT_f", [P, 2, T])
            lg = sb1("lg", [P, J, NG])
            lgd = sb1("lgd", [P, J, NG])
            gmx = sb1("gmx", [P, 2, J])
            cand = sb1("cand", [P, J, E])
            cm = sb1("cm", [P, 2, J])
            maskf = sb1("maskf", [P, 2, J, E])
            maskb = sb1("maskb", [P, 2, J, E], BF16)
            msum = sb1("msum", [P, E])
            tsum = sb1("tsum", [P, 2, E], BF16)
            tsumf = sb1("tsumf", [P, 2, E])
            gex = sb1("gex", [P, 2, J, NG])
            gsum = sb1("gsum", [P, 2, J])
            grec = sb1("grec", [P, 2, J])
            gc1 = sb1("gc1", [P, 2, J])
            lsel = sb1("lsel", [P, J, E])
            loc = sb1("loc", [P, J])
            keep = sb1("keep", [P, J])
            slo = sb1("slo", [P, 2, J])
            slot_i = sb1("slot_i", [P, 2, J], U32)

            w_loaded = sem1("w_loaded")
            res_loaded = sem("res_loaded")
            zeroed = sem1("zeroed")
            zero_set = sem1("zero_set")
            prep = sem1("prep")
            prep_g = sem1("prep_g")
            prep_mm = sem1("prep_mm")
            prep_w = sem1("prep_w")
            xt_loaded = [sem1(f"xt_loaded{i}") for i in range(2)]
            x_loaded = [sem1(f"x_loaded{i}") for i in range(2)]
            xtH_ready = sem1("xtH_ready")
            xtL_ready = sem1("xtL_ready")
            xb_ready = sem1("xb_ready")
            z_done = sem1("z_done")
            zH_ready = sem1("zH_ready")
            zL_ready = sem1("zL_ready")
            scores_done = sem1("scores_done")
            max_ready = sem1("max_ready")
            prob_ready = sem1("prob_ready")
            t_done = sem1("t_done")
            probT_ready = sem1("probT_ready")
            pv_done = sem1("pv_done")
            oT_ready = sem1("oT_ready")
            proj_done = sem1("proj_done")
            rinv_ready = sem1("rinv_ready")
            r1_ready = sem1("r1_ready")
            stats_ready = sem1("stats_ready")
            mom_step = sem1("mom_step")
            vq_ready = sem1("vq_ready")
            rs_ready = sem1("rs_ready")
            srt_ready = sem1("srt_ready")
            s_ready = sem1("s_ready")
            xn_ready = sem1("xn_ready")
            xnT_done = sem1("xnT_done")
            xnH_ready = sem1("xnH_ready")
            xnL_ready = sem1("xnL_ready")
            xn_kept = [sem(f"xn_kept{i}") for i in range(2)]
            logit_done = sem1("logit_done")
            gate_step = sem1("gate_step")
            mask_ready = sem1("mask_ready")
            gex_ready = sem1("gex_ready")
            rank_done = sem1("rank_done")
            slot_step = sem1("slot_step")
            slot_ready = sem1("slot_ready")
            slot_kept = sem1("slot_kept")
            scattered = [sem(f"scattered{i}") for i in range(2)]

            GS = 12
            SS = 6
            W_DMAS = 14

            def real(b):
                return not isinstance(b, int) or 0 <= b < NB

            def wait(eng, s, n):
                if not isinstance(n, int) or n > 0:
                    eng.wait_ge(s, n)

            def schedule(eng, step):
                for i in range(5):
                    step(i, i % 2)
                with eng.Fori(0, (NB - 6) // 2) as n:
                    step(n * 2 + 5, 1)
                    step(n * 2 + 6, 0)
                for i in range(NB - 1, NB + 3):
                    step(i, i % 2)

            with nc.Block() as block:
                @block.sync
                def _(sp):
                    def load(b, u):
                        wait(sp, xtL_ready, b - 1)
                        sp.dma_start(xt_in[:, u], x_T[:, bass.ds(b * T, T)]).then_inc(xt_loaded[u], 16)
                        wait(sp, xb_ready, b - 1)
                        wait(sp, pv_done, b - 1)
                        sp.dma_start(x_in[:, u].rearrange("p j d -> p (j d)"),
                                     x_tok.rearrange("b (p j) d -> p b (j d)", j=J)[:, bass.ds(b, 1)])\
                            .then_inc(x_loaded[u], 16)

                    sp.dma_start(w_raw[:, 0], wqT).then_inc(w_loaded, 16)
                    sp.dma_start(w_raw[:, 1], wkT).then_inc(w_loaded, 16)
                    sp.dma_start(w_raw[:, 2], wvT).then_inc(w_loaded, 16)
                    sp.dma_start(w_raw[:, 3], w_proj).then_inc(w_loaded, 16)
                    for n, v in enumerate((b_q, b_v, ln_w, ln_b)):
                        sp.dma_start(vecs[:, n:n + 1], v.rearrange("(d a) -> d a", a=1)).then_inc(w_loaded, 16)
                    sp.dma_start(bproj_row[:], b_proj.rearrange("(a d) -> a d", a=1)).then_inc(w_loaded, 16)
                    sp.dma_start(gc_raw[:, 0:E], w_gate).then_inc(w_loaded, 16)
                    sp.dma_start(gc_raw[:, E:NG], w_coef).then_inc(w_loaded, 16)
                    sp.dma_start(cst[:], consts).then_inc(w_loaded, 16)
                    sp.dma_start(res_raw[:], res_w).then_inc(w_loaded, 16)
                    sp.dma_start(res_bcol[:], res_bT).then_inc(w_loaded, 16)
                    load(0, 0)
                    load(1, 1)
                    sp.dma_start(res_out[:], res_out_w.rearrange("(c p) d -> p c d", p=P)).then_inc(res_loaded, 16)
                    sp.dma_start(res_obcol[:], res_out_bT).then_inc(res_loaded, 16)
                    sp.dma_start(e_bcol[:], inter_bT).then_inc(res_loaded, 16)
                    sp.dma_start(e_obcol[:], output_bT).then_inc(res_loaded, 16)
                    sp.wait_ge(zero_set, 1)
                    for q in range(4):
                        sp.dma_start(slots_dram.rearrange("(q p r) d -> q p (r d)", q=4, p=P)[q],
                                     zero_t[:]).then_inc(zeroed, 16)
                    sp.dma_start(moe_dram[S:S + 1, :], zero_t[0:1, 0:D]).then_inc(zeroed, 16)

                    def step(i, u):
                        if real(i + 2):
                            load(i + 2, u)
                        if real(i - 2):
                            sp.wait_ge(xn_ready, (i - 2) * J + J)
                            sp.dma_start(xn_all[:, bass.ds(i - 2, 1)], xn[:, u].rearrange("p j d -> p (j d)"))\
                                .then_inc(xn_kept[u], 16)

                    for i in range(5):
                        step(i, i % 2)
                    with sp.Fori(0, (NB - 8) // 2) as n:
                        step(n * 2 + 5, 1)
                        step(n * 2 + 6, 0)
                    for i in range(NB - 3, NB + 3):
                        step(i, i % 2)
                    for k in range(2):
                        sp.wait_ge(xn_kept[k], 16 * NB // 2)

                @block.tensor
                def _(pe):
                    pe.wait_ge(w_loaded, 16 * W_DMAS)
                    pe.wait_ge(prep, 3)
                    pe.wait_ge(prep_g, 2)
                    pe.matmul(psum[0][:, 0:D], w_raw[:, 0], w_raw[:, 1], start=True, stop=True).then_inc(prep_mm, 1)
                    pe.matmul(psum[1][:, 0:1], w_raw[:, 1], vecs[:, 0:1], start=True, stop=True).then_inc(prep_mm, 1)
                    pe.matmul(psum[2][:, 0:D], w_raw[:, 2], w_raw[:, 3], start=True, stop=True).then_inc(prep_mm, 1)
                    pe.matmul(psum[3][:, 0:D], bv_b[:], w_raw[:, 3], start=True, stop=False)
                    pe.matmul(psum[3][:, 0:D], ones_row[:], bproj_row[:], start=False, stop=True).then_inc(prep_mm, 1)
                    pe.matmul(psum[4][:, 0:NG], lnb_b[:], gc_raw[:], start=True, stop=True).then_inc(prep_mm, 1)
                    for c in range(IC):
                        mm = pe.matmul(psum[5][:, c:c + 1], res_raw[:, c * P:(c + 1) * P], vecs[:, 3:4],
                                       start=True, stop=True)
                    mm.then_inc(prep_mm, 1)

                    def project(b, u):
                        pe.wait_ge(xtL_ready, b + 1)
                        if not isinstance(b, int) or b > 2:
                            pe.wait_ge(gate_step, (b - 3) * GS + 1)
                        pe.matmul(psum[7][:], aH[:], xtH[:, u], start=True, stop=False)
                        pe.matmul(psum[7][:], aL[:], xtH[:, u], start=False, stop=False)
                        pe.matmul(psum[7][:], aH[:], xtL[:, u], start=False, stop=True).then_inc(z_done, 1)

                    def scores(b, u):
                        pe.wait_ge(zL_ready, b + 1)
                        for j in range(J):
                            wait(pe, prob_ready, J * (b - 1) + j + 1)
                            q = slice(j * P, (j + 1) * P)
                            pe.matmul(psum[j][:], zH[:, u, q], xtH[:, u], start=True, stop=False)
                            pe.matmul(psum[j][:], zL[:, u, q], xtH[:, u], start=False, stop=False)
                            pe.matmul(psum[j][:], zH[:, u, q], xtL[:, u], start=False, stop=True)\
                                .then_inc(scores_done, 1)

                    def rank(b, u):
                        pe.wait_ge(mask_ready, b + 1)
                        R = psum[7][:, 0:J * E].rearrange("p (j e) -> p j e", j=J)
                        pe.wait_ge(zL_ready, min(b + 4, NB) if isinstance(b, int) else b + 4)
                        for k in range(J):
                            pe.matmul(R, upper_b[:], maskb[:, u, k:k + 1, :].broadcast_to([P, J, E]),
                                      start=(k == 0), stop=False, skip_group_check=True)
                        for k in range(J - 1):
                            for j in range(k + 1, J):
                                pe.matmul(R[:, j], ident_b[:], maskb[:, u, k, :], start=False, stop=False,
                                          skip_group_check=True)
                        pe.matmul(R, ones_b[:], tsum[:, u:u + 1, :].broadcast_to([P, J, E]),
                                  start=False, stop=True, skip_group_check=True).then_inc(rank_done, 1)

                    def values(b, u):
                        pe.wait_ge(probT_ready, J * (b + 1))
                        wait(pe, r1_ready, J * b)
                        for k in range(J):
                            mm = pe.matmul(psum[6][:], x_in[:, u, k], probT[:, u, k], start=(k == 0), stop=(k == J - 1))
                        mm.then_inc(pv_done, 1)

                    def turn_xn(b, u):
                        pe.wait_ge(xn_ready, J * (b + 1))
                        pe.wait_ge(zL_ready, min(b + 3, NB) if isinstance(b, int) else b + 3)
                        wait(pe, slot_step, SS * (b - 1) + 1)
                        for j in range(J):
                            mm = pe.transpose(psum[7][:, j * P:(j + 1) * P], xn[:, u, j], ident)
                        mm.then_inc(xnT_done, 1)

                    def turn_probs(b, u):
                        for j in range(J):
                            pe.wait_ge(prob_ready, J * b + j + 1)
                            wait(pe, probT_ready, J * b + j - 1)
                            for k in range(J):
                                mm = pe.transpose(psum[4 + j % 2][:, k * P:(k + 1) * P],
                                                  prob[:, j, k * P:(k + 1) * P], ident)
                            mm.then_inc(t_done, 1)

                    def logits(b, u):
                        pe.wait_ge(xnH_ready, b + 1)
                        for j in range(J):
                            q = slice(j * P, (j + 1) * P)
                            mm = pe.matmul(psum[7][:, j * NG:(j + 1) * NG], xnT_f[:, u, q], gc_w[:],
                                           start=True, stop=True)
                        mm.then_inc(logit_done, 1)

                    def out_proj(b, u):
                        pe.wait_ge(oT_ready, b + 1)
                        for j in range(J):
                            mm = pe.matmul(psum[6][:, j * D:(j + 1) * D], oT[:, j * P:(j + 1) * P], w_vp[:],
                                           start=True, stop=True)
                        mm.then_inc(proj_done, 1)

                    pe.wait_ge(prep, 12)
                    pe.wait_ge(prep_w, 1)
                    project(0, 0)

                    def step(i, u):
                        v = 1 - u
                        if real(i):
                            scores(i, u)
                        if real(i - 3):
                            rank(i - 3, v)
                        if real(i - 1):
                            values(i - 1, v)
                        if real(i - 2):
                            turn_xn(i - 2, u)
                        if real(i):
                            turn_probs(i, u)
                        if real(i - 2):
                            logits(i - 2, u)
                        if real(i - 1):
                            out_proj(i - 1, v)
                        if real(i + 1):
                            project(i + 1, v)

                    schedule(pe, step)

                @block.scalar
                def _(act):
                    def z_high(b, u):
                        act.wait_ge(z_done, b + 1)
                        wait(act, scores_done, J * (b - 1))
                        act.activation(zH[:, u], psum[7][:], ACT.Identity, bias=c_z[:]).then_inc(zH_ready, 1)

                    def exps(b, u):
                        for j in range(J):
                            act.wait_ge(max_ready, J * b + j + 1)
                            wait(act, t_done, J * (b - 1) + j + 1)
                            if j == 0:
                                wait(act, rinv_ready, b - 1)
                            act.activation(prob[:, j], psum[j][:], ACT.Exp, bias=nmax[:, u, j:j + 1],
                                           accum_out=rsum[:, u, j:j + 1]).then_inc(prob_ready, 1)

                    def o_copy(b, u):
                        act.wait_ge(pv_done, b + 1)
                        wait(act, proj_done, b)
                        act.activation(oT[:], psum[6][:], ACT.Copy).then_inc(oT_ready, 1)

                    def probT_copy(b, u, j):
                        act.wait_ge(t_done, J * b + j + 1)
                        wait(act, pv_done, b - 1)
                        act.activation(probT[:, u, :, j * P:(j + 1) * P],
                                       psum[4 + j % 2][:].rearrange("p (k q) -> p k q", k=J), ACT.Copy)\
                            .then_inc(probT_ready, 1)

                    def xn_high(b, u):
                        act.wait_ge(xnT_done, b + 1)
                        wait(act, logit_done, b - 1)
                        wait(act, xnL_ready, b - 1)
                        act.activation(xnT_f[:, u], psum[7][:], ACT.Copy).then_inc(xnH_ready, 1)

                    def gate_exp(b, u):
                        act.wait_ge(gate_step, GS * b + 4)
                        wait(act, gate_step, GS * (b - 1))
                        act.activation(gex[:, u], lgd[:], ACT.Exp).then_inc(gex_ready, 1)

                    act.wait_ge(prep, 12)
                    z_high(0, 0)

                    def step(i, u):
                        v = 1 - u
                        if real(i):
                            exps(i, u)
                        if real(i - 1):
                            o_copy(i - 1, v)
                        if real(i):
                            probT_copy(i, u, 0)
                        if real(i - 2):
                            xn_high(i - 2, u)
                        if real(i):
                            probT_copy(i, u, 1)
                            probT_copy(i, u, 2)
                            probT_copy(i, u, 3)
                        if real(i - 2):
                            gate_exp(i - 2, u)
                        if real(i + 1):
                            z_high(i + 1, v)

                    schedule(act, step)

                @block.vector
                def _(ve):
                    ve.memset(ones_b[:], 1.0).then_inc(prep, 1)
                    ve.memset(ones_row[:], 1.0).then_inc(prep, 1)
                    ve.memset(expo[:], -0.5).then_inc(prep, 1)
                    ve.wait_ge(w_loaded, 16 * W_DMAS)
                    ve.tensor_copy(ident_b[:], ident).then_inc(prep, 1)
                    ve.tensor_copy(upper_b[:], cst[:, P:2 * P]).then_inc(prep, 1)
                    ve.tensor_scalar(gc_w[:], gc_raw[:], vecs[:, 2:3], None, ALU.mult).then_inc(prep, 1)
                    ve.wait_ge(prep_mm, 1)
                    scale = float(D) ** -0.5
                    ve.tensor_scalar(a_f[:], psum[0][:, 0:D], scale, None, ALU.mult).then_inc(prep, 1)
                    ve.wait_ge(prep, 7)
                    ve.tensor_copy(aH[:], a_f[:]).then_inc(prep, 1)
                    ve.wait_ge(prep, 8)
                    ve.tensor_tensor(aL[:], a_f[:], aH[:].bitcast(F32), ALU.subtract).then_inc(prep, 1)
                    ve.wait_ge(prep_mm, 6)
                    ve.tensor_scalar(c_z[:], psum[1][:, 0:1], scale, None, ALU.mult).then_inc(prep, 1)
                    ve.tensor_copy(w_vp[:], psum[2][:, 0:D]).then_inc(prep, 1)
                    ve.tensor_copy(b_vp[:], psum[3][:, 0:D]).then_inc(prep, 1)
                    ve.tensor_copy(gc_bias[:], psum[4][:, 0:NG]).then_inc(prep_w, 1)
                    ve.tensor_tensor(res_bias[:], psum[5][:, 0:IC], res_bcol[:], ALU.add).then_inc(prep_w, 1)
                    ve.tensor_scalar(res_s[:], res_raw[:], vecs[:, 2:3], None, ALU.mult).then_inc(prep_w, 1)
                    ve.wait_ge(prep_w, 3)
                    ve.tensor_copy(resH[:], res_s[:]).then_inc(prep_w, 1)
                    ve.wait_ge(prep_w, 4)
                    ve.tensor_tensor(resL[:], res_s[:], resH[:].bitcast(F32), ALU.subtract).then_inc(prep_w, 1)
                    ve.memset(tsum[:, 0], 0.0).then_inc(prep_w, 1)
                    ve.memset(tsumf[:, 0], 0.0).then_inc(prep_w, 1)
                    ve.wait_ge(prep_w, 7)

                    def x_high(b, u):
                        ve.wait_ge(xt_loaded[u], half(b) * 16)
                        wait(ve, scores_done, J * (b - 1))
                        ve.tensor_copy(xtH[:, u], xt_in[:, u]).then_inc(xtH_ready, 1)

                    def half(b):
                        return b // 2 + 1

                    def z_low(b, u):
                        ve.wait_ge(zH_ready, b + 1)
                        wait(ve, scores_done, J * (b - 1))
                        ve.scalar_tensor_tensor(zL[:, u], psum[7][:], c_z[:], zH[:, u].bitcast(F32),
                                                ALU.add, ALU.subtract).then_inc(zL_ready, 1)

                    def maxes(b, u):
                        for j in range(J):
                            ve.wait_ge(scores_done, J * b + j + 1)
                            wait(ve, prob_ready, J * (b - 2) + j + 1)
                            ve.tensor_reduce(nmax[:, u, j:j + 1], psum[j][:], AX.X, ALU.max, negate=True)\
                                .then_inc(max_ready, 1)

                    def slots(b, u):
                        s0 = SS * b
                        R = psum[7][:, 0:J * E].rearrange("p (j e) -> p j e", j=J)
                        ve.wait_ge(rank_done, b + 1)
                        wait(ve, slot_step, s0)
                        ve.tensor_tensor(lsel[:], R, maskf[:, u], ALU.mult).then_inc(slot_step, 1)
                        ve.wait_ge(slot_step, s0 + 1)
                        ve.tensor_reduce(loc[:], lsel[:], AX.X, ALU.add).then_inc(slot_step, 1)
                        ve.wait_ge(slot_step, s0 + 2)
                        ve.tensor_scalar(keep[:], loc[:], float(CAP), None, ALU.is_lt).then_inc(slot_step, 1)
                        ve.scalar_tensor_tensor(slo[:, 0], cm[:, u], -float(CAP), loc[:], ALU.mult, ALU.add)\
                            .then_inc(slot_step, 1)
                        ve.wait_ge(slot_step, s0 + 4)
                        ve.tensor_tensor(slo[:, 1], slo[:, 0], keep[:], ALU.mult).then_inc(slot_step, 1)
                        ve.tensor_tensor(coef_all[:, bass.ds(b, 1), J:2 * J], gc1[:, u], keep[:], ALU.mult)\
                            .then_inc(slot_step, 1)
                        ve.wait_ge(slot_step, s0 + 5)
                        wait(ve, scattered[u], scat(b))
                        wait(ve, slot_kept, b - 1)
                        ve.tensor_scalar(slot_i[:, u], slo[:, 1], float(S), None, ALU.add).then_inc(slot_ready, 1)

                    def scat(b):
                        return (b // 2) * 16 * J

                    def x_norm(b, u):
                        ve.wait_ge(prob_ready, J * (b + 1))
                        wait(ve, r1_ready, J * b)
                        ve.reciprocal(rinv[:], rsum[:, u]).then_inc(rinv_ready, 1)
                        ve.wait_ge(rinv_ready, b + 1)
                        ve.wait_ge(proj_done, b + 1)
                        ve.wait_ge(xb_ready, b + 1)
                        for j in range(J):
                            ve.scalar_tensor_tensor(r1[:, u, j], psum[6][:, j * D:(j + 1) * D], rinv[:, j:j + 1],
                                                    xb[:, u, j], ALU.mult, ALU.add).then_inc(r1_ready, 1)
                        wait(ve, mom_step, MS * b)
                        for j in range(J):
                            ve.wait_ge(r1_ready, J * b + j + 1)
                            ve.bn_stats(stats[:, j], r1[:, u, j]).then_inc(stats_ready, 1)
                        ve.wait_ge(stats_ready, J * (b + 1))
                        moments(ve, stats, mom, mean[:, u], var, mom_step, MS * b, lambda: wait(ve, xn_ready, J * (b - 1)))
                        ve.wait_ge(mom_step, MS * b + MS)
                        wait(ve, s_ready, b - 1)
                        ve.tensor_scalar(vq[:, u, 0], var[:], LN_EPS, None, ALU.add).then_inc(vq_ready, 1)
                        ve.tensor_scalar(vq[:, u, 1], var[:], 1.0 + GATE_LN_EPS, GATE_LN_EPS * LN_EPS,
                                         ALU.mult, ALU.add).then_inc(vq_ready, 1)
                        ve.tensor_scalar(vq[:, u, 2], var[:], 2 * (1.0 + GATE_LN_EPS), 2 * GATE_LN_EPS * LN_EPS,
                                         ALU.mult, ALU.add).then_inc(vq_ready, 1)

                    def x_norm2(b, u):
                        ve.wait_ge(rs_ready, b + 1)
                        wait(ve, xnT_done, b - 1)
                        wait(ve, xn_kept[u], (b // 2) * 16)
                        wait(ve, scattered[u], scat(b))
                        for j in range(J):
                            ve.tensor_scalar(xn[:, u, j], r1[:, u, j], mean[:, u, j:j + 1], rs[:, u, 1, j:j + 1],
                                             ALU.subtract, ALU.mult).then_inc(xn_ready, 1)

                    def xn_low(b, u):
                        ve.wait_ge(xnH_ready, b + 1)
                        ve.tensor_copy(xnH_all[:, bass.ds(b, 1)], xnT_f[:, u:u + 1]).then_inc(xnL_half, 1)
                        ve.wait_ge(xnL_half, b + 1)
                        ve.tensor_tensor(xnL_all[:, bass.ds(b, 1)], xnT_f[:, u:u + 1],
                                         xnH_all[:, bass.ds(b, 1)].bitcast(F32), ALU.subtract).then_inc(xnL_ready, 1)

                    def gate(b, u):
                        g0 = GS * b

                        def after(n):
                            ve.wait_ge(gate_step, g0 + n)

                        ve.wait_ge(logit_done, b + 1)
                        wait(ve, gate_step, g0)
                        ve.tensor_tensor(lg[:], psum[7][:, 0:J * NG].rearrange("p (j e) -> p j e", j=J),
                                         gc_bias[:].rearrange("p (a e) -> p a e", a=1).broadcast_to([P, J, NG]),
                                         ALU.add).then_inc(gate_step, 1)
                        after(1)
                        ve.tensor_reduce(gmx[:, 0], lg[:, :, 0:E], AX.X, ALU.max).then_inc(gmx_ready, 1)
                        ve.tensor_reduce(gmx[:, 1], lg[:, :, E:NG], AX.X, ALU.max).then_inc(gate_step, 1)
                        ve.wait_ge(gmx_ready, b + 1)
                        after(2)
                        wait(ve, gex_ready, b)
                        ve.tensor_tensor(lgd[:, :, 0:E], lg[:, :, 0:E],
                                         gmx[:, 0].rearrange("p (j a) -> p j a", a=1).broadcast_to([P, J, E]),
                                         ALU.subtract).then_inc(gate_step, 1)
                        ve.tensor_tensor(lgd[:, :, E:NG], lg[:, :, E:NG],
                                         gmx[:, 1].rearrange("p (j a) -> p j a", a=1).broadcast_to([P, J, 2]),
                                         ALU.subtract).then_inc(gate_step, 1)
                        after(3)
                        ve.scalar_tensor_tensor(cand[:], lgd[:, :, 0:E], 0.0, desc, ALU.is_ge, ALU.mult)\
                            .then_inc(gate_step, 1)
                        after(5)
                        wait(ve, slot_step, SS * (b - 1))
                        ve.tensor_reduce(cm[:, u], cand[:], AX.X, ALU.max).then_inc(gate_step, 1)
                        after(6)
                        wait(ve, rank_done, b - 1)
                        ve.tensor_tensor(maskf[:, u], desc,
                                         cm[:, u].rearrange("p (j a) -> p j a", a=1).broadcast_to([P, J, E]),
                                         ALU.is_equal).then_inc(gate_step, 1)
                        after(7)
                        ve.tensor_copy(maskb[:, u], maskf[:, u]).then_inc(mask_ready, 1)
                        ve.tensor_reduce(msum[:], maskf[:, u].rearrange("p j e -> p e j"), AX.X, ALU.add)\
                            .then_inc(gate_step, 1)
                        after(8)
                        wait(ve, rank_done, b)
                        ve.tensor_tensor(tsumf[:, 1 - u], tsumf[:, u], msum[:], ALU.add).then_inc(gate_step, 1)
                        after(9)
                        ve.tensor_copy(tsum[:, 1 - u], tsumf[:, 1 - u]).then_inc(gate_step, 1)

                    def gate2(b, u):
                        g0 = GS * b
                        ve.wait_ge(gex_ready, b + 1)
                        wait(ve, gc_ready, 2 * b)
                        ve.tensor_reduce(gsum[:, 0], gex[:, u, :, 0:E], AX.X, ALU.add).then_inc(gsum_ready, 1)
                        ve.tensor_reduce(gsum[:, 1], gex[:, u, :, E:NG], AX.X, ALU.add).then_inc(gsum_ready, 1)
                        ve.wait_ge(gsum_ready, 2 * b + 2)
                        ve.reciprocal(grec[:], gsum[:]).then_inc(gate_step, 1)
                        ve.wait_ge(gate_step, g0 + 11)
                        wait(ve, slot_step, SS * (b - 1))
                        ve.tensor_tensor(gc1t[:], grec[:, 0], grec[:, 1], ALU.mult).then_inc(gc_ready, 1)
                        ve.wait_ge(gc_ready, 2 * b + 1)
                        ve.tensor_tensor(gc1[:, u], gc1t[:], gex[:, u, :, E + 1], ALU.mult).then_inc(gc_ready, 1)
                        ve.tensor_tensor(coef_all[:, bass.ds(b, 1), 0:J], gex[:, u, :, E], grec[:, 1], ALU.mult)\
                            .then_inc(gate_step, 1)

                    x_high(0, 0)
                    z_low(0, 0)
                    x_high(1, 1)

                    def step(i, u):
                        v = 1 - u
                        if real(i):
                            maxes(i, u)
                        if real(i - 3):
                            slots(i - 3, v)
                        if real(i - 2):
                            xn_low(i - 2, u)
                        if real(i - 2):
                            gate(i - 2, u)
                        if real(i - 1):
                            x_norm(i - 1, v)
                        if real(i + 1):
                            z_low(i + 1, v)
                        if real(i - 2):
                            gate2(i - 2, u)
                        if real(i - 1):
                            x_norm2(i - 1, v)
                        if real(i + 2):
                            x_high(i + 2, u)

                    xnL_half = sem1("xnL_half")
                    gmx_ready = sem1("gmx_ready")
                    gsum_ready = sem1("gsum_ready")
                    gc_ready = sem1("gc_ready")
                    gc1t = sb1("gc1t", [P, J])
                    for i in range(5):
                        step(i, i % 2)
                    with ve.Fori(0, (NB - 8) // 2) as n:
                        step(n * 2 + 5, 1)
                        step(n * 2 + 6, 0)
                    for i in range(NB - 3, NB + 3):
                        step(i, i % 2)
                    ve.wait_ge(slot_step, SS * NB)
                    ve.wait_ge(gate_step, GS * NB)

                @block.gpsimd
                def _(po):
                    po.memset(zero_t[:], 0.0).then_inc(zero_set, 1)
                    po.wait_ge(w_loaded, 16 * W_DMAS)
                    po.tensor_copy(bv_b[:], vecs[:, 1:2].broadcast_to([P, P])).then_inc(prep_g, 1)
                    po.tensor_copy(lnb_b[:], vecs[:, 3:4].broadcast_to([P, P])).then_inc(prep_g, 1)
                    po.wait_ge(prep, 12)

                    def x_low(b, u):
                        po.wait_ge(xtH_ready, b + 1)
                        wait(po, scores_done, J * (b - 1))
                        po.tensor_tensor(xtL[:, u], xt_in[:, u], xtH[:, u].bitcast(F32), ALU.subtract)\
                            .then_inc(xtL_ready, 1)

                    def x_bias(b, u):
                        po.wait_ge(x_loaded[u], (b // 2 + 1) * 16)
                        wait(po, r1_ready, J * (b - 1))
                        po.tensor_tensor(xb[:, u], x_in[:, u],
                                         b_vp[:].rearrange("p (a d) -> p a d", a=1).broadcast_to([P, J, D]),
                                         ALU.add).then_inc(xb_ready, 1)

                    def factors(b, u):
                        po.wait_ge(vq_ready, 3 * b + 3)
                        wait(po, xn_ready, J * (b - 1))
                        po.tensor_tensor(rs[:, u], vq[:, u, 0:2], expo[:].rearrange("p (a j) -> p a j", a=2), ALU.pow)\
                            .then_inc(rs_ready, 1)
                        po.wait_ge(rs_ready, b + 1)
                        wait(po, s_ready, b)
                        po.tensor_tensor(srt[:], vq[:, u, 2], rs[:, u, 1], ALU.mult).then_inc(srt_ready, 1)
                        po.wait_ge(srt_ready, b + 1)
                        po.tensor_tensor(coef_all[:, bass.ds(b, 1), 2 * J:3 * J], srt[:], rs[:, u, 0], ALU.mult)\
                            .then_inc(s_ready, 1)

                    def scatter(b, u):
                        po.wait_ge(slot_ready, b + 1)
                        po.tensor_copy(slot_all[:, bass.ds(b, 1)], slot_i[:, u:u + 1]).then_inc(slot_kept, 1)
                        for j in range(J):
                            po.indirect_dma_start(out=slots_dram,
                                                  out_offset=bass.IndirectOffsetOnAxis(ap=slot_i[:, u, j:j + 1], axis=0),
                                                  in_=xn[:, u, j], in_offset=None, bounds_check=S - 1,
                                                  oob_is_err=False).then_inc(scattered[u], 16)

                    x_low(0, 0)
                    x_bias(0, 0)
                    x_low(1, 1)
                    x_bias(1, 1)

                    po.wait_ge(zeroed, 80)

                    def step(i, u):
                        v = 1 - u
                        if real(i - 3):
                            scatter(i - 3, v)
                        if real(i - 1):
                            factors(i - 1, v)
                        if real(i + 2):
                            x_low(i + 2, u)
                            x_bias(i + 2, u)

                    for i in range(5):
                        step(i, i % 2)
                    with po.Fori(0, (NB - 8) // 2) as n:
                        step(n * 2 + 5, 1)
                        step(n * 2 + 6, 0)
                    for i in range(NB - 3, NB + 3):
                        step(i, i % 2)
                    po.wait_ge(s_ready, NB)
                    po.wait_ge(slot_kept, NB)
                    for k in range(2):
                        po.wait_ge(scattered[k], 16 * J * NB // 2)

        with ExitStack() as c2:
            def sb2(name, shape, dt=F32):
                return c2.enter_context(nc.sbuf_tensor(name, shape, dt))

            def sem2(name):
                return c2.enter_context(nc.semaphore(name))

            wi_in = sb2("wi_in", [P, 2, I])
            wi_s = sb2("wi_s", [P, I])
            wiH = sb2("wiH", [P, 2, I], F32R)
            wiL = sb2("wiL", [P, 2, I], F32R)
            wo = sb2("wo", [P, 2, IC, D])
            hb = sb2("hb", [P, 2, IC])
            ob = sb2("ob", [P, 2])
            s_in = sb2("s_in", [P, 2, J, D])
            sT = sb2("sT", [P, T])
            sH = sb2("sH", [P, 2, T], F32R)
            sL = sb2("sL", [P, 2, T], F32R)
            h = sb2("h", [P, 2, IC, T])
            eT = sb2("eT", [P, T])
            e_out = sb2("e_out", [P, 2, J, D])

            wi_loaded = [sem2(f"wi_loaded{i}") for i in range(2)]
            wo_loaded = [sem2(f"wo_loaded{i}") for i in range(2)]
            s_loaded = [sem2(f"s_loaded{i}") for i in range(2)]
            e_stored = [sem2(f"e_stored{i}") for i in range(2)]
            ws_ready = sem2("ws_ready")
            wiH_ready = sem2("wiH_ready")
            wiL_ready = sem2("wiL_ready")
            hb_done = sem2("hb_done")
            hb_ready = sem2("hb_ready")
            sT_done = sem2("sT_done")
            sH_ready = sem2("sH_ready")
            sL_ready = sem2("sL_ready")
            in_done = sem2("in_done")
            h_ready = sem2("h_ready")
            out_done = sem2("out_done")
            eT_ready = sem2("eT_ready")
            back_done = sem2("back_done")
            e_ready = sem2("e_ready")
            NT = E * TPE
            slots_t = slots_dram.rearrange("(t p j) d -> p t (j d)", p=P, j=J)
            moe_t = moe_dram[0:S, :].rearrange("(t p j) d -> p t (j d)", p=P, j=J)
            inter_v = inter_w.rearrange("e d i -> d e i")
            output_v = output_w.rearrange("e (c p) d -> p e c d", p=P)

            def real(t):
                return not isinstance(t, int) or 0 <= t < NT

            def wait(eng, s, n):
                if not isinstance(n, int) or n > 0:
                    eng.wait_ge(s, n)

            def schedule(eng, step):
                for t in range(4):
                    step(t, t // 2, t)
                with eng.Fori(0, (NT - 8) // 4) as n:
                    for k in range(4):
                        step(n * 4 + (4 + k), n * 2 + (2 + k // 2), k)
                for t in range(NT - 4, NT + 1):
                    step(t, t // 2, t % 4)

            with nc.Block() as block:
                @block.sync
                def _(sp):
                    def weights(e, w):
                        wait(sp, ws_ready, e - 1)
                        wait(sp, hb_done, e - 1)
                        sp.dma_start(wi_in[:, w], inter_v[:, bass.ds(e, 1)]).then_inc(wi_loaded[w], 16)
                        wait(sp, out_done, TPE * (e - 1))
                        sp.dma_start(wo[:, w].rearrange("p c d -> p 1 c d") if False else wo[:, w:w + 1],
                                     output_v[:, bass.ds(e, 1)]).then_inc(wo_loaded[w], 16)

                    def tile(t, u):
                        wait(sp, sT_done, t - 1)
                        sp.dma_start(s_in[:, u].rearrange("p j d -> p (j d)"), slots_t[:, bass.ds(t, 1)])\
                            .then_inc(s_loaded[u], 16)

                    weights(0, 0)
                    weights(1, 1)
                    tile(0, 0)
                    tile(1, 1)

                    def step(t, e, k):
                        if real(t + 2):
                            tile(t + 2, k % 2)
                        if k % 2 == 1 and (not isinstance(e, int) or e + 2 < E):
                            weights(e + 2, k // 2)
                        if real(t - 1):
                            sp.wait_ge(e_ready, t)
                            sp.dma_start(moe_t[:, bass.ds(t - 1, 1)], e_out[:, 1 - k % 2].rearrange("p j d -> p (j d)"))\
                                .then_inc(e_stored[1 - k % 2], 16)

                    for t in range(4):
                        step(t, t // 2, t)
                    with sp.Fori(0, (NT - 8) // 4) as n:
                        for k in range(4):
                            step(n * 4 + (4 + k), n * 2 + (2 + k // 2), k)
                    for t in range(NT - 4, NT + 1):
                        step(t, t // 2, t % 4)
                    for k in range(2):
                        sp.wait_ge(e_stored[k], 16 * NT // 2)

                @block.tensor
                def _(pe):
                    def turn(t, k):
                        pe.wait_ge(s_loaded[k % 2], (t // 2 + 1) * 16)
                        wait(pe, sH_ready, t)
                        for j in range(J):
                            mm = pe.transpose(psum[0][:, j * P:(j + 1) * P], s_in[:, k % 2, j], ident)
                        mm.then_inc(sT_done, 1)

                    def bias(e, w):
                        pe.wait_ge(wi_loaded[w], (e // 2 + 1) * 16)
                        wait(pe, hb_ready, e)
                        for c in range(IC):
                            mm = pe.matmul(psum[1][:, c:c + 1], wi_in[:, w, c * P:(c + 1) * P], vecs[:, 3:4],
                                           start=True, stop=True)
                        mm.then_inc(hb_done, 1)

                    def up(t, e, k, c):
                        w = k // 2
                        if c == 0:
                            pe.wait_ge(sL_ready, t + 1)
                            pe.wait_ge(wiL_ready, e + 1)
                        wait(pe, h_ready, IC * t + c - 1)
                        q = slice(c * P, (c + 1) * P)
                        o = psum[2 + c % 2][:]
                        pe.matmul(o, wiH[:, w, q], sH[:, k % 2], start=True, stop=False)
                        pe.matmul(o, wiL[:, w, q], sH[:, k % 2], start=False, stop=False)
                        pe.matmul(o, wiH[:, w, q], sL[:, k % 2], start=False, stop=True).then_inc(in_done, 1)

                    def down(t, e, k, c):
                        if c == 0:
                            pe.wait_ge(wo_loaded[k // 2], (e // 2 + 1) * 16)
                            wait(pe, eT_ready, t)
                        pe.wait_ge(h_ready, IC * t + c + 1)
                        mm = pe.matmul(psum[4][:], wo[:, k // 2, c], h[:, k % 2, c], start=(c == 0), stop=(c == IC - 1))
                        if c == IC - 1:
                            mm.then_inc(out_done, 1)

                    def back(t, k):
                        pe.wait_ge(eT_ready, t + 1)
                        wait(pe, e_ready, t)
                        for j in range(J):
                            mm = pe.transpose(psum[5][:, j * P:(j + 1) * P], eT[:, j * P:(j + 1) * P], ident)
                        mm.then_inc(back_done, 1)

                    bias(0, 0)
                    turn(0, 0)

                    def step(t, e, k):
                        pk = (k - 1) % 4
                        pe_ = e if k % 2 else e - 1
                        if real(t + 1):
                            if k % 2 == 0 and (not isinstance(e, int) or e + 1 < E):
                                bias(e + 1, 1 - k // 2)
                            turn(t + 1, (k + 1) % 4)
                        for c in range(IC):
                            if real(t):
                                up(t, e, k, c)
                            if real(t - 1):
                                down(t - 1, pe_, pk, c)
                            if c == 1 and real(t - 2):
                                back(t - 2, (k - 2) % 4)
                        if isinstance(t, int) and t == NT:
                            back(t - 1, pk)

                    schedule(pe, step)

                @block.scalar
                def _(act):
                    def gelus(t, e, k):
                        for c in range(IC):
                            act.wait_ge(in_done, IC * t + c + 1)
                            if c == 0:
                                act.wait_ge(hb_ready, e + 1)
                                wait(act, out_done, t - 1)
                            act.activation(h[:, k % 2, c], psum[2 + c % 2][:], ACT.Gelu_apprx_tanh,
                                           bias=hb[:, k // 2, c:c + 1]).then_inc(h_ready, 1)

                    def e_bias(t, w):
                        act.wait_ge(out_done, t + 1)
                        wait(act, back_done, t)
                        act.activation(eT[:], psum[4][:], ACT.Identity, bias=ob[:, w:w + 1]).then_inc(eT_ready, 1)

                    def s_copy(t):
                        act.wait_ge(sT_done, t + 1)
                        wait(act, sL_ready, t)
                        act.activation(sT[:], psum[0][:], ACT.Copy).then_inc(sH_ready, 1)

                    s_copy(0)

                    def step(t, e, k):
                        if real(t + 1):
                            s_copy(t + 1)
                        if real(t):
                            gelus(t, e, k)
                        if real(t - 1):
                            e_bias(t - 1, (k - 1) % 4 // 2)

                    schedule(act, step)

                @block.vector
                def _(ve):
                    def prepare(e, w):
                        ve.wait_ge(wi_loaded[w], (e // 2 + 1) * 16)
                        wait(ve, wiL_ready, e)
                        ve.tensor_scalar(wi_s[:], wi_in[:, w], vecs[:, 2:3], None, ALU.mult).then_inc(ws_ready, 1)
                        ve.wait_ge(ws_ready, e + 1)
                        wait(ve, in_done, IC * TPE * (e - 1))
                        ve.tensor_copy(wiH[:, w], wi_s[:]).then_inc(wiH_ready, 1)
                        ve.wait_ge(wiH_ready, e + 1)
                        ve.tensor_tensor(wiL[:, w], wi_s[:], wiH[:, w].bitcast(F32), ALU.subtract).then_inc(wiL_ready, 1)
                        ve.wait_ge(hb_done, e + 1)
                        wait(ve, h_ready, IC * TPE * (e - 1))
                        wait(ve, eT_ready, TPE * (e - 1))
                        ve.tensor_copy(ob[:, w:w + 1], e_obcol[:, bass.ds(e, 1)]).then_inc(ob_ready, 1)
                        ve.wait_ge(ob_ready, e + 1)
                        ve.tensor_tensor(hb[:, w:w + 1], psum[1][:, 0:IC], e_bcol[:, bass.ds(e, 1)], ALU.add)\
                            .then_inc(hb_ready, 1)

                    def s_split(t, u):
                        ve.wait_ge(sH_ready, t + 1)
                        wait(ve, in_done, IC * (t - 1))
                        ve.tensor_copy(sH[:, u], sT[:]).then_inc(sHr, 1)
                        ve.wait_ge(sHr, t + 1)
                        ve.tensor_tensor(sL[:, u], sT[:], sH[:, u].bitcast(F32), ALU.subtract).then_inc(sL_ready, 1)

                    def e_copy(t, u):
                        ve.wait_ge(back_done, t + 1)
                        wait(ve, e_stored[u], (t // 2) * 16)
                        ve.tensor_copy(e_out[:, u].rearrange("p j d -> p (j d)"), psum[5][:]).then_inc(e_ready, 1)

                    sHr = sem2("sHr")
                    ob_ready = sem2("ob_ready")
                    prepare(0, 0)
                    s_split(0, 0)

                    def step(t, e, k):
                        if k % 2 == 0 and (not isinstance(e, int) or e + 1 < E):
                            prepare(e + 1, 1 - k // 2)
                        if real(t + 1):
                            s_split(t + 1, 1 - k % 2)
                        if real(t - 2):
                            e_copy(t - 2, k % 2)
                        if isinstance(t, int) and t == NT:
                            e_copy(t - 1, 1 - k % 2)

                    schedule(ve, step)

        with ExitStack() as c3:
            def sb3(name, shape, dt=F32):
                return c3.enter_context(nc.sbuf_tensor(name, shape, dt))

            def sem3(name):
                return c3.enter_context(nc.semaphore(name))

            h2 = sb3("h2", [P, 2, IC, T])
            rT = sb3("rT", [P, T])
            idx = sb3("idx", [P, 2, J], U32)
            coef = sb3("coef", [P, 2, 3 * J])
            moe = sb3("moe", [P, 2, J, D])
            y0 = sb3("y0", [P, 2, J, D])
            y1 = sb3("y1", [P, J, D])
            y2 = sb3("y2", [P, 2, J, D])
            st2 = sb3("st2", [P, J, 6])
            mom2 = sb3("mom2", [P, J, 3])
            mean2 = sb3("mean2", [P, 2, J])
            var2 = sb3("var2", [P, J])
            ve2 = sb3("ve2", [P, 2, J])
            rs2 = sb3("rs2", [P, 2, J])
            res = sb3("res", [P, 2, J, D])

            in2_done = sem3("in2_done")
            h2_ready = sem3("h2_ready")
            out2_done = sem3("out2_done")
            rT_ready = sem3("rT_ready")
            back2_done = sem3("back2_done")
            idx_ready = sem3("idx_ready")
            coef_ready = sem3("coef_ready")
            gathered = [sem3(f"gathered{i}") for i in range(2)]
            y0_ready = sem3("y0_ready")
            y1_ready = sem3("y1_ready")
            y2_ready = sem3("y2_ready")
            st2_ready = sem3("st2_ready")
            mom2_step = sem3("mom2_step")
            ve2_ready = sem3("ve2_ready")
            rs2_ready = sem3("rs2_ready")
            res_ready = sem3("res_ready")
            stored = [sem3(f"stored{i}") for i in range(2)]
            out_v = out.rearrange("b (p j) d -> p b (j d)", j=J)

            def real(b):
                return not isinstance(b, int) or 0 <= b < NB

            def schedule(eng, step):
                for b in range(4):
                    step(b, b % 2)
                with eng.Fori(0, (NB - 6) // 2) as n:
                    step(n * 2 + 4, 0)
                    step(n * 2 + 5, 1)
                for b in range(NB - 2, NB + 3):
                    step(b, b % 2)

            with nc.Block() as block:
                @block.tensor
                def _(pe):
                    def up(b, u, c):
                        wait(pe, h2_ready, IC * b + c - 1)
                        q = slice(c * P, (c + 1) * P)
                        o = psum[2 + c % 2][:]
                        xh = xnH_all[:, bass.ds(b, 1)]
                        xl = xnL_all[:, bass.ds(b, 1)]
                        pe.matmul(o, resH[:, q], xh, start=True, stop=False)
                        pe.matmul(o, resL[:, q], xh, start=False, stop=False)
                        pe.matmul(o, resH[:, q], xl, start=False, stop=True).then_inc(in2_done, 1)

                    def down(b, u, c):
                        if c == 0:
                            wait(pe, rT_ready, b)
                        pe.wait_ge(h2_ready, IC * b + c + 1)
                        mm = pe.matmul(psum[4][:], res_out[:, c], h2[:, u, c], start=(c == 0), stop=(c == IC - 1))
                        if c == IC - 1:
                            mm.then_inc(out2_done, 1)

                    def back(b, u):
                        pe.wait_ge(rT_ready, b + 1)
                        wait(pe, y1_ready, J * (b - 1))
                        for j in range(J):
                            mm = pe.transpose(psum[5 + u][:, j * P:(j + 1) * P], rT[:, j * P:(j + 1) * P], ident)
                        mm.then_inc(back2_done, 1)

                    pe.wait_ge(res_loaded, 64)

                    def step(b, u):
                        for c in range(IC):
                            if real(b):
                                up(b, u, c)
                            if real(b - 1):
                                down(b - 1, 1 - u, c)
                            if c == 1 and real(b - 2):
                                back(b - 2, u)

                    schedule(pe, step)

                @block.scalar
                def _(act):
                    def step(b, u):
                        if real(b):
                            for c in range(IC):
                                act.wait_ge(in2_done, IC * b + c + 1)
                                wait(act, out2_done, b - 1)
                                act.activation(h2[:, u, c], psum[2 + c % 2][:], ACT.Gelu_apprx_tanh,
                                               bias=res_bias[:, c:c + 1]).then_inc(h2_ready, 1)
                        if real(b - 1):
                            act.wait_ge(out2_done, b)
                            wait(act, back2_done, b - 1)
                            act.activation(rT[:], psum[4][:], ACT.Identity, bias=res_obcol[:]).then_inc(rT_ready, 1)

                    act.wait_ge(res_loaded, 64)
                    schedule(act, step)

                @block.gpsimd
                def _(po):
                    def gather(b, u):
                        wait(po, gathered[u], (b // 2) * 16 * J)
                        po.tensor_copy(idx[:, u:u + 1], slot_all[:, bass.ds(b, 1)]).then_inc(idx_ready, 1)
                        wait(po, y1_ready, J * (b - 1))
                        wait(po, y2_ready, J * (b - 1))
                        po.wait_ge(idx_ready, b + 1)
                        wait(po, y0_ready, b - 1)
                        po.tensor_copy(coef[:, u:u + 1], coef_all[:, bass.ds(b, 1)]).then_inc(coef_ready, 1)
                        for j in range(J):
                            po.indirect_dma_start(out=moe[:, u, j], out_offset=None, in_=moe_dram,
                                                  in_offset=bass.IndirectOffsetOnAxis(ap=idx[:, u, j:j + 1], axis=0),
                                                  bounds_check=S, oob_is_err=False).then_inc(gathered[u], 16)

                    def weigh(b, u):
                        po.wait_ge(coef_ready, b + 1)
                        po.wait_ge(gathered[u], (b // 2 + 1) * 16 * J)
                        wait(po, y1_ready, J * (b - 1))
                        po.tensor_tensor(y0[:, u], moe[:, u],
                                         coef[:, u, J:2 * J].rearrange("p (j a) -> p j a", a=1).broadcast_to([P, J, D]),
                                         ALU.mult).then_inc(y0_ready, 1)

                    def factor(b, u):
                        po.wait_ge(ve2_ready, b + 1)
                        wait(po, res_ready, J * (b - 1))
                        po.tensor_tensor(rs2[:, u], ve2[:, u], expo[:, 0:J], ALU.pow).then_inc(rs2_ready, 1)

                    gather(0, 0)
                    gather(1, 1)

                    def step(b, u):
                        if real(b):
                            weigh(b, u)
                        if real(b - 2):
                            factor(b - 2, u)
                        if real(b + 2):
                            gather(b + 2, u)

                    for b in range(4):
                        step(b, b % 2)
                    with po.Fori(0, (NB - 6) // 2) as n:
                        step(n * 2 + 4, 0)
                        step(n * 2 + 5, 1)
                    for b in range(NB - 2, NB + 3):
                        step(b, b % 2)

                @block.vector
                def _(ve):
                    def total(b, u):
                        ve.wait_ge(back2_done, b + 1)
                        ve.wait_ge(y0_ready, b + 1)
                        wait(ve, y2_ready, J * b)
                        for j in range(J):
                            ve.scalar_tensor_tensor(y1[:, j], psum[5 + u][:, j * D:(j + 1) * D], coef[:, u, j:j + 1],
                                                    y0[:, u, j], ALU.mult, ALU.add).then_inc(y1_ready, 1)
                        wait(ve, res_ready, J * (b - 1))
                        for j in range(J):
                            ve.wait_ge(y1_ready, J * b + j + 1)
                            ve.scalar_tensor_tensor(y2[:, u, j], xn_all[:, bass.ds(b, 1), j * D:(j + 1) * D],
                                                    coef[:, u, 2 * J + j:2 * J + j + 1], y1[:, j],
                                                    ALU.mult, ALU.add).then_inc(y2_ready, 1)
                        wait(ve, mom2_step, MS * b)
                        for j in range(J):
                            ve.wait_ge(y2_ready, J * b + j + 1)
                            ve.bn_stats(st2[:, j], y2[:, u, j]).then_inc(st2_ready, 1)
                        ve.wait_ge(st2_ready, J * (b + 1))
                        moments(ve, st2, mom2, mean2[:, u], var2, mom2_step, MS * b, lambda: wait(ve, res_ready, J * (b - 1)))
                        ve.wait_ge(mom2_step, MS * b + MS)
                        wait(ve, rs2_ready, b - 1)
                        ve.tensor_scalar(ve2[:, u], var2[:], LN_EPS, None, ALU.add).then_inc(ve2_ready, 1)

                    def norm(b, u):
                        ve.wait_ge(rs2_ready, b + 1)
                        wait(ve, stored[u], (b // 2) * 16)
                        for j in range(J):
                            ve.tensor_scalar(res[:, u, j], y2[:, u, j], mean2[:, u, j:j + 1], rs2[:, u, j:j + 1],
                                             ALU.subtract, ALU.mult).then_inc(res_ready, 1)

                    def step(b, u):
                        if real(b - 2):
                            total(b - 2, u)
                        if real(b - 3):
                            norm(b - 3, 1 - u)

                    schedule(ve, step)

                @block.sync
                def _(sp):
                    def step(b, u):
                        if real(b - 3):
                            sp.wait_ge(res_ready, J * (b - 2))
                            sp.dma_start(out_v[:, bass.ds(b - 3, 1)], res[:, 1 - u].rearrange("p j d -> p (j d)"))\
                                .then_inc(stored[1 - u], 16)

                    schedule(sp, step)
                    for k in range(2):
                        sp.wait_ge(stored[k], 16 * NB // 2)


_OUT = (16, 512, 128)


def kernel(**inputs):
    import numpy as np
    import concourse.bacc as bacc
    from concourse.bass_utils import run_bass_kernel_spmd

    a = {k.removeprefix("L0_"): np.asarray(v) for k, v in inputs.items()}
    x = a["attn_x"]
    NB, T, D = x.shape
    P_, J = 128, T // 128
    E, _, I = a["ffn_inter_w"].shape
    w = a["attn_w_qkv"]
    c = np.ascontiguousarray
    consts = np.zeros((P_, 2 * P_ + J * E), np.float32)
    consts[:, :P_] = np.eye(P_)
    consts[:, P_:2 * P_] = np.triu(np.ones((P_, P_)), 1)
    consts[:, 2 * P_:] = np.tile(E - np.arange(E), J)
    arrays = {
        "x_tok": c(x),
        "x_T": c(x.reshape(NB, P_, J, D).transpose(3, 0, 2, 1).reshape(D, NB * T)),
        "wqT": c(w[:, :D].T), "wkT": c(w[:, D:2 * D].T), "wvT": c(w[:, 2 * D:].T),
        "w_proj": c(a["attn_w_proj"]),
        "b_q": c(a["attn_b_qkv"][:D]), "b_v": c(a["attn_b_qkv"][2 * D:]), "b_proj": c(a["attn_b_proj"]),
        "ln_w": c(a["ffn_attn_nw"]), "ln_b": c(a["ffn_attn_nb"]),
        "w_gate": c(a["ffn_wg"]), "w_coef": c(a["ffn_res_coef"]),
        "inter_w": c(a["ffn_inter_w"]),
        "inter_bT": c(a["ffn_inter_b"].reshape(E, I // P_, P_).transpose(2, 0, 1)),
        "output_w": c(a["ffn_output_w"]), "output_bT": c(a["ffn_output_b"].T),
        "res_w": c(a["ffn_res_inter_w"]), "res_bT": c(a["ffn_res_inter_b"].reshape(I // P_, P_).T),
        "res_out_w": c(a["ffn_res_output_w"]), "res_out_bT": c(a["ffn_res_output_b"].reshape(D, 1)),
        "consts": consts,
    }
    nc = bacc.Bacc("TRN2", target_bir_lowering=False, num_devices=1)
    args = {n: nc.dram_tensor(n, v.shape, mybir.dt.from_np(v.dtype), kind="ExternalInput").ap()
            for n, v in arrays.items()}
    out = nc.dram_tensor("out", _OUT, F32, kind="ExternalOutput").ap()
    build(nc, *args.values(), out)
    r = run_bass_kernel_spmd(nc, [arrays], core_ids=[0])
    return r.results[0]["out"]
```

```python
from contextlib import ExitStack

import concourse.bass as bass
from concourse import mybir

F32 = mybir.dt.float32
F32R = mybir.dt.float32r
BF16 = mybir.dt.bfloat16
U32 = mybir.dt.uint32
ALU = mybir.AluOpType
ACT = mybir.ActivationFunctionType
AX = mybir.AxisListType

P = 128
LN_EPS = 1e-5
GATE_LN_EPS = 1e-12


def build(nc, x_tok, x_T, wqT, wkT, wvT, w_proj, b_q, b_v, b_proj, ln_w, ln_b, w_gate, w_coef, inter_w, inter_bT,
          output_w, output_bT, res_w, res_bT, res_out_w, res_out_bT, consts, out):
    NB, T, D = x_tok.shape
    J = T // P
    E, _, I = inter_w.shape
    IC = I // P
    S = NB * T
    CAP = max(4, -(-S // E))
    TPE = CAP // T
    NG = E + 2
    assert D == P and J == 4 and TPE == 2 and NB % 2 == 0

    slots_dram = nc.dram_tensor("slots_dram", [S, D], F32).ap()
    moe_dram = nc.dram_tensor("moe_dram", [S + 1, D], F32).ap()

    MS = 4

    def moments(ve, stats, mom, var, steps, done):
        ve.tensor_reduce(mom[:, :, 0:2], stats[:].rearrange("p j (h f) -> p j f h", h=2)[:, :, 1:3], AX.X, ALU.add)\
            .then_inc(steps, 1)
        ve.tensor_tensor(mom[:, :, 2], stats[:, :, 1], stats[:, :, 4], ALU.subtract).then_inc(steps, 1)
        ve.wait_ge(steps, done + 2)
        ve.scalar_tensor_tensor(var[:], mom[:, :, 2], 0.25, mom[:, :, 2], ALU.mult, ALU.mult).then_inc(steps, 1)
        ve.wait_ge(steps, done + 3)
        ve.scalar_tensor_tensor(var[:], mom[:, :, 1], 1.0 / D, var[:], ALU.mult, ALU.add).then_inc(steps, 1)

    with ExitStack() as ctx:
        def sb(name, shape, dt=F32):
            return ctx.enter_context(nc.sbuf_tensor(name, shape, dt))

        def sem(name):
            return ctx.enter_context(nc.semaphore(name))

        res_loaded = sem("res_loaded")
        w_raw = sb("w_raw", [P, 4, D])
        vecs = sb("vecs", [P, 4])
        bproj_row = sb("bproj_row", [1, D])
        gc_raw = sb("gc_raw", [P, NG])
        gc_w = sb("gc_w", [P, NG])
        gc_bias = sb("gc_bias", [P, NG])
        cst = sb("cst", [P, 2 * P + J * E])
        ident_b = sb("ident_b", [P, P], BF16)
        upper_b = sb("upper_b", [P, P], BF16)
        ones_b = sb("ones_b", [P, P], BF16)
        ones_row = sb("ones_row", [1, P])
        bv_b = sb("bv_b", [P, P])
        lnb_b = sb("lnb_b", [P, P])
        expo = sb("expo", [P, 3 * J])
        coef_mul = sb("coef_mul", [P, J, 4])
        a_f = sb("a_f", [P, D])
        aH = sb("aH", [P, D], F32R)
        aL = sb("aL", [P, D], F32R)
        c_z = sb("c_z", [P, 1])
        w_vp = sb("w_vp", [P, D])
        b_vp = sb("b_vp", [P, D])
        zero_t = sb("zero_t", [P, 2048])
        res_raw = sb("res_raw", [P, I])
        res_s = sb("res_s", [P, I])
        resH = sb("resH", [P, I], F32R)
        resL = sb("resL", [P, I], F32R)
        res_bias = sb("res_bias", [P, IC])
        res_bcol = sb("res_bcol", [P, IC])
        res_out = sb("res_out", [P, IC, D])
        res_obcol = sb("res_obcol", [P, 1])
        e_bcol = sb("e_bcol", [P, E, IC])
        e_obcol = sb("e_obcol", [P, E])
        ident = cst[:, 0:P]
        desc = cst[:, 2 * P:2 * P + J * E].rearrange("p (j e) -> p j e", j=J)

        kept = sb("kept", [P, NB, 2, T])
        slot_all = sb("slot_all", [P, NB, J], U32)
        coef_all = sb("coef_all", [P, NB, J, 4])

        psum = [ctx.enter_context(nc.psum_tensor(f"bank{i}", [P, 512], F32)) for i in range(8)]

        with ExitStack() as c1:
            def sb1(name, shape, dt=F32):
                return c1.enter_context(nc.sbuf_tensor(name, shape, dt))

            def sem1(name):
                return c1.enter_context(nc.semaphore(name))

            xt_in = sb1("xt_in", [P, 2, T])
            x_in = sb1("x_in", [P, 2, J, D])
            xtH = sb1("xtH", [P, 2, T], F32R)
            xtL = sb1("xtL", [P, 2, T], F32R)
            xb = sb1("xb", [P, 2, J, D])
            zH = sb1("zH", [P, 2, T], F32R)
            zL = sb1("zL", [P, 2, T], F32R)
            nmax = sb1("nmax", [P, 2, J])
            rsum = sb1("rsum", [P, 2, J])
            rinv = sb1("rinv", [P, J])
            prob = sb1("prob", [P, J, T])
            probT = sb1("probT", [P, 2, J, T])
            oT = sb1("oT", [P, T])
            r1 = sb1("r1", [P, 2, J, D])
            stats = sb1("stats", [P, J, 6])
            mom = sb1("mom", [P, J, 3])
            var = sb1("var", [P, J])
            vq = sb1("vq", [P, 2, 3, J])
            rs = sb1("rs", [P, 2, 3, J])
            nb = sb1("nb", [P, 2, J])
            xn_both = sb1("xn_both", [P, 2, 2, T])
            xn = xn_both[:, :, 0].rearrange("p u (j d) -> p u j d", j=J)
            xnT = xn_both[:, :, 1]
            lg = sb1("lg", [P, J, NG])
            lgd = sb1("lgd", [P, J, NG])
            gmx = sb1("gmx", [P, 2, J])
            cand = sb1("cand", [P, J, E])
            cm = sb1("cm", [P, 2, J])
            maskb = sb1("maskb", [P, 2, J, E], BF16)
            tsum = sb1("tsum", [P, 2, J, E], BF16)
            gex = sb1("gex", [P, 2, J, NG])
            gsum = sb1("gsum", [P, 2, J])
            grec = sb1("grec", [P, 2, J])
            cg = sb1("cg", [P, 2, J])
            lsel = sb1("lsel", [P, J, E])
            loc = sb1("loc", [P, J])
            slo = sb1("slo", [P, 2, J])
            slot_i = sb1("slot_i", [P, 2, J], U32)

            w_loaded = sem1("w_loaded")
            zeroed = sem1("zeroed")
            zero_set = sem1("zero_set")
            prep = sem1("prep")
            prep_g = sem1("prep_g")
            prep_mm = sem1("prep_mm")
            prep_w = sem1("prep_w")
            xt_loaded = [sem1(f"xt_loaded{i}") for i in range(2)]
            x_loaded = [sem1(f"x_loaded{i}") for i in range(2)]
            xtH_ready = sem1("xtH_ready")
            xtL_ready = sem1("xtL_ready")
            xb_ready = sem1("xb_ready")
            z_done = sem1("z_done")
            zH_ready = sem1("zH_ready")
            zL_ready = sem1("zL_ready")
            scores_done = sem1("scores_done")
            max_ready = sem1("max_ready")
            prob_ready = sem1("prob_ready")
            t_done = sem1("t_done")
            probT_ready = sem1("probT_ready")
            pv_done = sem1("pv_done")
            oT_ready = sem1("oT_ready")
            proj_done = sem1("proj_done")
            rinv_ready = sem1("rinv_ready")
            r1_ready = sem1("r1_ready")
            stats_ready = sem1("stats_ready")
            mom_step = sem1("mom_step")
            vq_ready = sem1("vq_ready")
            rs_ready = sem1("rs_ready")
            nb_ready = sem1("nb_ready")
            s_ready = sem1("s_ready")
            xn_ready = sem1("xn_ready")
            xnT_done = sem1("xnT_done")
            xnT_ready = sem1("xnT_ready")
            xn_kept = [sem(f"xn_kept{i}") for i in range(2)]
            logit_done = sem1("logit_done")
            gate_step = sem1("gate_step")
            mask_ready = sem1("mask_ready")
            gex_ready = sem1("gex_ready")
            rank_done = sem1("rank_done")
            slot_step = sem1("slot_step")
            slot_ready = sem1("slot_ready")
            slot_kept = sem1("slot_kept")
            scattered = [sem(f"scattered{i}") for i in range(2)]

            GS = 13
            SS = 5
            W_DMAS = 14
            LAST = 3

            def real(b):
                return not isinstance(b, int) or 0 <= b < NB

            def wait(eng, s, n):
                if not isinstance(n, int) or n > 0:
                    eng.wait_ge(s, n)

            def schedule(eng, step):
                for i in range(5):
                    step(i, i % 2)
                with eng.Fori(0, (NB - 8) // 2) as n:
                    step(n * 2 + 5, 1)
                    step(n * 2 + 6, 0)
                for i in range(NB - 3, NB + LAST):
                    step(i, i % 2)

            with nc.Block() as block:
                @block.sync
                def _(sp):
                    def load_xt(b, u):
                        wait(sp, xtL_ready, b - 1)
                        sp.dma_start(xt_in[:, u], x_T[:, bass.ds(b * T, T)]).then_inc(xt_loaded[u], 16)

                    def load_x(b, u):
                        wait(sp, xb_ready, b - 1)
                        wait(sp, pv_done, b - 1)
                        sp.dma_start(x_in[:, u].rearrange("p j d -> p (j d)"),
                                     x_tok.rearrange("b (p j) d -> p b (j d)", j=J)[:, bass.ds(b, 1)])\
                            .then_inc(x_loaded[u], 16)

                    load_xt(0, 0)
                    sp.dma_start(w_raw[:, 0], wqT).then_inc(w_loaded, 16)
                    sp.dma_start(w_raw[:, 1], wkT).then_inc(w_loaded, 16)
                    sp.dma_start(w_raw[:, 2], wvT).then_inc(w_loaded, 16)
                    sp.dma_start(w_raw[:, 3], w_proj).then_inc(w_loaded, 16)
                    sp.dma_start(cst[:], consts).then_inc(w_loaded, 16)
                    sp.dma_start(res_raw[:], res_w).then_inc(w_loaded, 16)
                    sp.dma_start(res_bcol[:], res_bT).then_inc(w_loaded, 16)
                    load_x(0, 0)
                    load_xt(1, 1)
                    sp.wait_ge(zero_set, 1)
                    for q in range(4):
                        sp.dma_start(slots_dram.rearrange("(q p r) d -> q p (r d)", q=4, p=P)[q],
                                     zero_t[:]).then_inc(zeroed, 16)
                    sp.dma_start(moe_dram[S:S + 1, :], zero_t[0:1, 0:D]).then_inc(zeroed, 16)
                    load_xt(2, 0)

                    def step(i, u):
                        v = 1 - u
                        if real(i + 3):
                            load_xt(i + 3, v)
                        if real(i + 1):
                            load_x(i + 1, v)
                        if real(i - 2):
                            sp.wait_ge(xnT_ready, i - 1)
                            sp.dma_start(kept[:, bass.ds(i - 2, 1)], xn_both[:, u]).then_inc(xn_kept[u], 16)

                    schedule(sp, step)
                    for k in range(2):
                        sp.wait_ge(xn_kept[k], 16 * NB // 2)

                @block.tensor
                def _(pe):
                    pe.wait_ge(w_loaded, 16 * W_DMAS)
                    pe.wait_ge(prep, 2)
                    pe.wait_ge(prep_g, 7)
                    pe.matmul(psum[0][:, 0:D], w_raw[:, 0], w_raw[:, 1], start=True, stop=True).then_inc(prep_mm, 1)
                    pe.matmul(psum[1][:, 0:1], w_raw[:, 1], vecs[:, 0:1], start=True, stop=True).then_inc(prep_mm, 1)
                    pe.matmul(psum[2][:, 0:D], w_raw[:, 2], w_raw[:, 3], start=True, stop=True).then_inc(prep_mm, 1)
                    pe.matmul(psum[3][:, 0:D], bv_b[:], w_raw[:, 3], start=True, stop=False)
                    pe.matmul(psum[3][:, 0:D], ones_row[:], bproj_row[:], start=False, stop=True).then_inc(prep_mm, 1)
                    pe.matmul(psum[4][:, 0:NG], lnb_b[:], gc_raw[:], start=True, stop=True).then_inc(prep_mm, 1)
                    for c in range(IC):
                        mm = pe.matmul(psum[5][:, c:c + 1], res_raw[:, c * P:(c + 1) * P], vecs[:, 3:4],
                                       start=True, stop=True)
                    mm.then_inc(prep_mm, 1)

                    def scores(b, u):
                        pe.wait_ge(zL_ready, b + 1)
                        for j in range(J):
                            wait(pe, prob_ready, J * (b - 1) + j + 1)
                            q = slice(j * P, (j + 1) * P)
                            pe.matmul(psum[j][:], zH[:, u, q], xtH[:, u], start=True, stop=False)
                            pe.matmul(psum[j][:], zL[:, u, q], xtH[:, u], start=False, stop=False)
                            pe.matmul(psum[j][:], zH[:, u, q], xtL[:, u], start=False, stop=True)\
                                .then_inc(scores_done, 1)

                    def values(b, u):
                        pe.wait_ge(x_loaded[u], (b // 2 + 1) * 16)
                        pe.wait_ge(probT_ready, J * (b + 1))
                        wait(pe, r1_ready, J * b)
                        for k in range(J):
                            mm = pe.matmul(psum[6][:], x_in[:, u, k], probT[:, u, k], start=(k == 0), stop=(k == J - 1))
                        mm.then_inc(pv_done, 1)

                    def rank(b, u):
                        pe.wait_ge(mask_ready, b + 1)
                        pe.wait_ge(gate_step, GS * b + 1)
                        R = psum[7][:, 0:J * E].rearrange("p (j e) -> p j e", j=J)
                        for k in range(J):
                            pe.matmul(R, upper_b[:], maskb[:, u, k:k + 1, :].broadcast_to([P, J, E]),
                                      start=(k == 0), stop=False, skip_group_check=True)
                            pe.matmul(R, ones_b[:], tsum[:, u, k:k + 1, :].broadcast_to([P, J, E]),
                                      start=False, stop=False, skip_group_check=True)
                        for k in range(J - 1):
                            mm = pe.matmul(R[:, k + 1:J], ident_b[:],
                                           maskb[:, u, k:k + 1, :].broadcast_to([P, J - 1 - k, E]),
                                           start=False, stop=(k == J - 2), skip_group_check=True)
                        mm.then_inc(rank_done, 1)

                    def project(b, u):
                        pe.wait_ge(xtL_ready, b + 1)
                        wait(pe, prob_ready, J * (b - 1) + 1)
                        pe.matmul(psum[0][:], aH[:], xtH[:, u], start=True, stop=False)
                        pe.matmul(psum[0][:], aL[:], xtH[:, u], start=False, stop=False)
                        pe.matmul(psum[0][:], aH[:], xtL[:, u], start=False, stop=True).then_inc(z_done, 1)

                    def turn_xn(b, u):
                        pe.wait_ge(xn_ready, J * (b + 1))
                        wait(pe, slot_step, SS * (b - 1) + 1)
                        for j in range(J):
                            mm = pe.transpose(psum[7][:, j * P:(j + 1) * P], xn[:, u, j], ident)
                        mm.then_inc(xnT_done, 1)

                    def turn_probs(b, u):
                        for j in range(J):
                            pe.wait_ge(prob_ready, J * b + j + 1)
                            wait(pe, probT_ready, J * b + j - 1)
                            for k in range(J):
                                mm = pe.transpose(psum[4 + j % 2][:, k * P:(k + 1) * P],
                                                  prob[:, j, k * P:(k + 1) * P], ident)
                            mm.then_inc(t_done, 1)

                    def out_proj(b, u):
                        pe.wait_ge(oT_ready, b + 1)
                        for j in range(J):
                            mm = pe.matmul(psum[6][:, j * D:(j + 1) * D], oT[:, j * P:(j + 1) * P], w_vp[:],
                                           start=True, stop=True)
                        mm.then_inc(proj_done, 1)

                    def logits(b, u):
                        pe.wait_ge(xnT_ready, b + 1)
                        for j in range(J):
                            mm = pe.matmul(psum[7][:, j * NG:(j + 1) * NG], xnT[:, u, j * P:(j + 1) * P], gc_w[:],
                                           start=True, stop=True)
                        mm.then_inc(logit_done, 1)

                    pe.wait_ge(prep, 11)
                    project(0, 0)

                    def step(i, u):
                        v = 1 - u
                        if real(i):
                            scores(i, u)
                        if real(i - 1):
                            values(i - 1, v)
                        if real(i - 3):
                            rank(i - 3, v)
                        if real(i + 1):
                            project(i + 1, v)
                        if real(i - 2):
                            turn_xn(i - 2, u)
                        if real(i):
                            turn_probs(i, u)
                        if real(i - 1):
                            out_proj(i - 1, v)
                        if real(i - 2):
                            logits(i - 2, u)

                    schedule(pe, step)

                @block.scalar
                def _(act):
                    for n, v in enumerate((b_q, b_v, ln_w, ln_b)):
                        act.dma_start(vecs[:, n:n + 1], v.rearrange("(d a) -> d a", a=1)).then_inc(w_loaded, 16)
                    act.dma_start(bproj_row[:], b_proj.rearrange("(a d) -> a d", a=1)).then_inc(w_loaded, 16)
                    act.dma_start(gc_raw[:, 0:E], w_gate).then_inc(w_loaded, 16)
                    act.dma_start(gc_raw[:, E:NG], w_coef).then_inc(w_loaded, 16)
                    act.dma_start(res_out[:], res_out_w.rearrange("(c p) d -> p c d", p=P)).then_inc(res_loaded, 16)
                    act.dma_start(res_obcol[:], res_out_bT).then_inc(res_loaded, 16)
                    act.dma_start(e_bcol[:], inter_bT).then_inc(res_loaded, 16)
                    act.dma_start(e_obcol[:], output_bT).then_inc(res_loaded, 16)

                    def x_high(b, u):
                        act.wait_ge(xt_loaded[u], (b // 2 + 1) * 16)
                        wait(act, scores_done, J * (b - 1))
                        act.activation(xtH[:, u], xt_in[:, u], ACT.Copy).then_inc(xtH_ready, 1)

                    def z_high(b, u):
                        act.wait_ge(z_done, b + 1)
                        wait(act, scores_done, J * (b - 1))
                        act.activation(zH[:, u], psum[0][:], ACT.Identity, bias=c_z[:]).then_inc(zH_ready, 1)

                    def exps(b, u):
                        for j in range(J):
                            act.wait_ge(max_ready, J * b + j + 1)
                            wait(act, t_done, J * (b - 1) + j + 1)
                            if j == 0:
                                wait(act, rinv_ready, b - 1)
                            act.activation(prob[:, j], psum[j][:], ACT.Exp, bias=nmax[:, u, j:j + 1],
                                           accum_out=rsum[:, u, j:j + 1]).then_inc(prob_ready, 1)

                    def normalise(b, u):
                        act.wait_ge(nb_ready, b + 1)
                        wait(act, xnT_done, b - 1)
                        wait(act, xn_kept[u], (b // 2) * 16)
                        wait(act, scattered[u], (b // 2) * 16 * J)
                        for j in range(J):
                            act.activation(xn[:, u, j], r1[:, u, j], ACT.Identity, bias=nb[:, u, j:j + 1],
                                           scale=rs[:, u, 0, j:j + 1]).then_inc(xn_ready, 1)

                    def gate_exp(b, u):
                        act.wait_ge(gate_step, GS * b + 5)
                        wait(act, gate_step, GS * (b - 1))
                        act.activation(gex[:, u], lgd[:], ACT.Exp).then_inc(gex_ready, 1)

                    def o_copy(b, u):
                        act.wait_ge(pv_done, b + 1)
                        wait(act, proj_done, b)
                        act.activation(oT[:], psum[6][:], ACT.Copy).then_inc(oT_ready, 1)

                    def xnT_copy(b, u):
                        act.wait_ge(xnT_done, b + 1)
                        wait(act, logit_done, b - 1)
                        act.activation(xnT[:, u], psum[7][:], ACT.Copy).then_inc(xnT_ready, 1)

                    def probT_copy(b, u, j):
                        act.wait_ge(t_done, J * b + j + 1)
                        wait(act, pv_done, b - 1)
                        act.activation(probT[:, u, :, j * P:(j + 1) * P],
                                       psum[4 + j % 2][:].rearrange("p (k q) -> p k q", k=J), ACT.Copy)\
                            .then_inc(probT_ready, 1)

                    x_high(0, 0)
                    x_high(1, 1)
                    act.wait_ge(prep, 11)
                    z_high(0, 0)

                    def step(i, u):
                        v = 1 - u
                        if real(i):
                            exps(i, u)
                        if real(i - 2):
                            normalise(i - 2, u)
                        if real(i - 3):
                            gate_exp(i - 3, v)
                        if real(i + 2):
                            x_high(i + 2, u)
                        if real(i - 1):
                            o_copy(i - 1, v)
                        if real(i + 1):
                            z_high(i + 1, v)
                        if real(i - 2):
                            xnT_copy(i - 2, u)
                        if real(i):
                            for j in range(J):
                                probT_copy(i, u, j)

                    schedule(act, step)

                @block.vector
                def _(ve):
                    ve.memset(ones_b[:], 1.0).then_inc(prep, 1)
                    ve.memset(ones_row[:], 1.0).then_inc(prep, 1)
                    ve.wait_ge(w_loaded, 16 * W_DMAS)
                    ve.tensor_copy(ident_b[:], ident).then_inc(prep, 1)
                    ve.tensor_copy(upper_b[:], cst[:, P:2 * P]).then_inc(prep, 1)
                    ve.tensor_scalar(gc_w[:], gc_raw[:], vecs[:, 2:3], None, ALU.mult).then_inc(prep, 1)
                    ve.wait_ge(prep_mm, 1)
                    scale = float(D) ** -0.5
                    ve.tensor_scalar(a_f[:], psum[0][:, 0:D], scale, None, ALU.mult).then_inc(prep, 1)
                    ve.wait_ge(prep, 6)
                    ve.tensor_copy(aH[:], a_f[:]).then_inc(prep, 1)
                    ve.wait_ge(prep, 7)
                    ve.tensor_tensor(aL[:], a_f[:], aH[:].bitcast(F32), ALU.subtract).then_inc(prep, 1)
                    ve.wait_ge(prep_mm, 6)
                    ve.tensor_scalar(c_z[:], psum[1][:, 0:1], scale, None, ALU.mult).then_inc(prep, 1)
                    ve.tensor_copy(w_vp[:], psum[2][:, 0:D]).then_inc(prep, 1)
                    ve.tensor_copy(b_vp[:], psum[3][:, 0:D]).then_inc(prep, 1)
                    ve.tensor_copy(gc_bias[:], psum[4][:, 0:NG]).then_inc(prep_w, 1)
                    ve.tensor_tensor(res_bias[:], psum[5][:, 0:IC], res_bcol[:], ALU.add).then_inc(prep_w, 1)
                    ve.tensor_scalar(res_s[:], res_raw[:], vecs[:, 2:3], None, ALU.mult).then_inc(prep_w, 1)
                    ve.wait_ge(prep_w, 3)
                    ve.tensor_copy(resH[:], res_s[:]).then_inc(prep_w, 1)
                    ve.wait_ge(prep_w, 4)
                    ve.tensor_tensor(resL[:], res_s[:], resH[:].bitcast(F32), ALU.subtract).then_inc(prep_w, 1)
                    ve.memset(tsum[:, 0], 0.0).then_inc(prep_w, 1)
                    ve.wait_ge(prep_w, 6)

                    def z_low(b, u):
                        ve.wait_ge(zH_ready, b + 1)
                        wait(ve, scores_done, J * (b - 1))
                        ve.scalar_tensor_tensor(zL[:, u], psum[0][:], c_z[:], zH[:, u].bitcast(F32),
                                                ALU.add, ALU.subtract).then_inc(zL_ready, 1)

                    def row_max(b, u, j):
                        ve.wait_ge(scores_done, J * b + j + 1)
                        wait(ve, prob_ready, J * (b - 2) + j + 1)
                        ve.tensor_reduce(nmax[:, u, j:j + 1], psum[j][:], AX.X, ALU.max, negate=True)\
                            .then_inc(max_ready, 1)

                    def norm_bias(b, u):
                        ve.wait_ge(rs_ready, 2 * b + 1)
                        wait(ve, xn_ready, J * (b - 1))
                        ve.scalar_tensor_tensor(nb[:, u], mom[:, :, 0], -0.5, rs[:, u, 0], ALU.mult, ALU.mult)\
                            .then_inc(nb_ready, 1)

                    def slots(b, u):
                        s0 = SS * b
                        R = psum[7][:, 0:J * E].rearrange("p (j e) -> p j e", j=J)
                        ve.wait_ge(rank_done, b + 1)
                        wait(ve, slot_step, s0)
                        ve.tensor_tensor(lsel[:], R, maskb[:, u], ALU.mult).then_inc(slot_step, 1)
                        ve.wait_ge(slot_step, s0 + 1)
                        ve.tensor_reduce(loc[:], lsel[:], AX.X, ALU.add).then_inc(slot_step, 1)
                        ve.wait_ge(slot_step, s0 + 2)
                        ve.scalar_tensor_tensor(slo[:, 0], cm[:, u], -float(CAP), loc[:], ALU.mult, ALU.add)\
                            .then_inc(slot_step, 1)
                        ve.wait_ge(gate_step, GS * (b + 1))
                        ve.scalar_tensor_tensor(coefs(b, 2), loc[:], float(CAP), cg[:, u], ALU.is_lt, ALU.mult)\
                            .then_inc(slot_step, 1)
                        ve.wait_ge(slot_step, s0 + 3)
                        ve.scalar_tensor_tensor(slo[:, 1], loc[:], float(CAP), slo[:, 0], ALU.is_lt, ALU.mult)\
                            .then_inc(slot_step, 1)
                        ve.wait_ge(slot_step, s0 + 5)
                        wait(ve, scattered[u], (b // 2) * 16 * J)
                        wait(ve, slot_kept, b - 1)
                        ve.tensor_scalar(slot_i[:, u], slo[:, 1], float(S), None, ALU.add).then_inc(slot_ready, 1)

                    def x_norm(b, u):
                        ve.wait_ge(prob_ready, J * (b + 1))
                        wait(ve, r1_ready, J * b)
                        ve.reciprocal(rinv[:], rsum[:, u]).then_inc(rinv_ready, 1)
                        ve.wait_ge(rinv_ready, b + 1)
                        ve.wait_ge(proj_done, b + 1)
                        ve.wait_ge(xb_ready, b + 1)
                        wait(ve, xn_ready, J * (b - 1))
                        for j in range(J):
                            ve.scalar_tensor_tensor(r1[:, u, j], psum[6][:, j * D:(j + 1) * D], rinv[:, j:j + 1],
                                                    xb[:, u, j], ALU.mult, ALU.add).then_inc(r1_ready, 1)
                        wait(ve, mom_step, MS * b)
                        for j in range(J):
                            ve.wait_ge(r1_ready, J * b + j + 1)
                            ve.bn_stats(stats[:, j], r1[:, u, j]).then_inc(stats_ready, 1)
                        ve.wait_ge(stats_ready, J * (b + 1))
                        wait(ve, nb_ready, b)
                        moments(ve, stats, mom, var, mom_step, MS * b)
                        ve.wait_ge(mom_step, MS * b + MS)
                        wait(ve, s_ready, b - 1)
                        ve.tensor_scalar(vq[:, u, 0:2],
                                         var[:].rearrange("p (a j) -> p a j", a=1).broadcast_to([P, 2, J]),
                                         1.0 + GATE_LN_EPS, GATE_LN_EPS * LN_EPS, ALU.mult, ALU.add)\
                            .then_inc(vq_ready, 1)
                        ve.tensor_scalar(vq[:, u, 2], var[:], LN_EPS, None, ALU.add).then_inc(vq_ready, 1)

                    def coefs(b, n):
                        return coef_all[:, bass.ds(b, 1), :, n]

                    def spread(t, n):
                        return t.rearrange("p (j a) -> p j a", a=1).broadcast_to([P, J, n])

                    def gate(b, u):
                        g0 = GS * b

                        def after(n):
                            ve.wait_ge(gate_step, g0 + n)

                        ve.wait_ge(logit_done, b + 1)
                        wait(ve, gate_step, g0)
                        ve.tensor_tensor(lg[:], psum[7][:, 0:J * NG].rearrange("p (j e) -> p j e", j=J),
                                         gc_bias[:].rearrange("p (a e) -> p a e", a=1).broadcast_to([P, J, NG]),
                                         ALU.add).then_inc(gate_step, 1)
                        after(1)
                        ve.tensor_reduce(gmx[:, 0], lg[:, :, 0:E], AX.X, ALU.max).then_inc(gate_step, 1)
                        ve.tensor_reduce(gmx[:, 1], lg[:, :, E:NG], AX.X, ALU.max).then_inc(gate_step, 1)
                        after(2)
                        wait(ve, gex_ready, b)
                        ve.tensor_tensor(lgd[:, :, 0:E], lg[:, :, 0:E], spread(gmx[:, 0], E), ALU.subtract)\
                            .then_inc(gate_step, 1)
                        after(3)
                        ve.tensor_tensor(lgd[:, :, E:NG], lg[:, :, E:NG], spread(gmx[:, 1], 2), ALU.subtract)\
                            .then_inc(gate_step, 1)
                        after(4)
                        ve.scalar_tensor_tensor(cand[:], lgd[:, :, 0:E], 0.0, desc, ALU.is_ge, ALU.mult)\
                            .then_inc(gate_step, 1)
                        after(6)
                        wait(ve, slot_step, SS * (b - 1))
                        ve.tensor_reduce(cm[:, u], cand[:], AX.X, ALU.max).then_inc(gate_step, 1)
                        after(7)
                        wait(ve, rank_done, b - 1)
                        ve.tensor_tensor(maskb[:, u], desc, spread(cm[:, u], E), ALU.is_equal)\
                            .then_inc(mask_ready, 1)
                        ve.wait_ge(mask_ready, b + 1)
                        wait(ve, rank_done, b)
                        ve.tensor_tensor(tsum[:, 1 - u], tsum[:, u], maskb[:, u], ALU.add).then_inc(gate_step, 1)

                    def gate_coefs(b, u):
                        g0 = GS * b
                        ve.wait_ge(gex_ready, b + 1)
                        ve.tensor_reduce(gsum[:, 0], gex[:, u, :, 0:E], AX.X, ALU.add).then_inc(gate_step, 1)
                        ve.tensor_reduce(gsum[:, 1], gex[:, u, :, E:NG], AX.X, ALU.add).then_inc(gate_step, 1)
                        ve.wait_ge(gate_step, g0 + 10)
                        ve.reciprocal(grec[:], gsum[:]).then_inc(gate_step, 1)
                        ve.wait_ge(gate_step, g0 + 11)
                        ve.tensor_tensor(coef_all[:, bass.ds(b, 1), :, 0:2], gex[:, u, :, E:NG], spread(grec[:, 1], 2),
                                         ALU.mult).then_inc(gate_step, 1)
                        ve.wait_ge(gate_step, g0 + 12)
                        wait(ve, slot_step, SS * (b - 1))
                        ve.tensor_tensor(cg[:, u], coefs(b, 1), grec[:, 0], ALU.mult).then_inc(gate_step, 1)

                    z_low(0, 0)

                    def step(i, u):
                        v = 1 - u
                        if real(i):
                            row_max(i, u, 0)
                            row_max(i, u, 1)
                        if real(i - 2):
                            norm_bias(i - 2, u)
                        if real(i):
                            row_max(i, u, 2)
                            row_max(i, u, 3)
                        if real(i - 3):
                            gate(i - 3, v)
                            gate_coefs(i - 3, v)
                            slots(i - 3, v)
                        if real(i + 1):
                            z_low(i + 1, v)
                        if real(i - 1):
                            x_norm(i - 1, v)

                    schedule(ve, step)
                    ve.wait_ge(slot_step, SS * NB)
                    ve.wait_ge(gate_step, GS * NB)

                @block.gpsimd
                def _(po):
                    po.memset(zero_t[:], 0.0).then_inc(zero_set, 1)
                    po.memset(expo[:, 0:J], -0.5).then_inc(prep_g, 1)
                    po.memset(expo[:, J:2 * J], 0.5).then_inc(prep_g, 1)
                    po.memset(expo[:, 2 * J:3 * J], -0.5).then_inc(prep_g, 1)
                    po.memset(coef_mul[:], 1.0).then_inc(prep_g, 1)
                    po.wait_ge(prep_g, 4)
                    po.memset(coef_mul[:, :, 3], 2.0).then_inc(prep_g, 1)
                    po.wait_ge(w_loaded, 16 * W_DMAS)
                    po.tensor_copy(bv_b[:], vecs[:, 1:2].broadcast_to([P, P])).then_inc(prep_g, 1)
                    po.tensor_copy(lnb_b[:], vecs[:, 3:4].broadcast_to([P, P])).then_inc(prep_g, 1)
                    po.wait_ge(prep_g, 7)

                    def x_low(b, u):
                        po.wait_ge(xtH_ready, b + 1)
                        wait(po, scores_done, J * (b - 1))
                        po.tensor_tensor(xtL[:, u], xt_in[:, u], xtH[:, u].bitcast(F32), ALU.subtract)\
                            .then_inc(xtL_ready, 1)

                    def x_bias(b, u):
                        po.wait_ge(x_loaded[u], (b // 2 + 1) * 16)
                        wait(po, r1_ready, J * (b - 1))
                        po.tensor_tensor(xb[:, u], x_in[:, u],
                                         b_vp[:].rearrange("p (a d) -> p a d", a=1).broadcast_to([P, J, D]),
                                         ALU.add).then_inc(xb_ready, 1)

                    def factors(b, u):
                        po.wait_ge(vq_ready, 2 * b + 2)
                        wait(po, xn_ready, J * (b - 1))
                        po.tensor_tensor(rs[:, u, 0], vq[:, u, 0], expo[:, 0:J], ALU.pow).then_inc(rs_ready, 1)
                        wait(po, s_ready, b - 1)
                        po.tensor_tensor(rs[:, u, 1:3], vq[:, u, 1:3],
                                         expo[:, J:3 * J].rearrange("p (a j) -> p a j", a=2), ALU.pow)\
                            .then_inc(rs_ready, 1)
                        po.wait_ge(rs_ready, 2 * b + 2)
                        po.tensor_tensor(coef_all[:, bass.ds(b, 1), :, 3], rs[:, u, 1], rs[:, u, 2], ALU.mult)\
                            .then_inc(s_ready, 1)

                    def scatter(b, u):
                        if isinstance(b, int) and b == 0:
                            po.wait_ge(zeroed, 80)
                        po.wait_ge(slot_ready, b + 1)
                        po.tensor_copy(slot_all[:, bass.ds(b, 1)], slot_i[:, u:u + 1]).then_inc(slot_kept, 1)
                        for j in range(J):
                            po.indirect_dma_start(out=slots_dram,
                                                  out_offset=bass.IndirectOffsetOnAxis(ap=slot_i[:, u, j:j + 1], axis=0),
                                                  in_=xn[:, u, j], in_offset=None, bounds_check=S - 1,
                                                  oob_is_err=False).then_inc(scattered[u], 16)

                    x_low(0, 0)
                    x_low(1, 1)
                    po.wait_ge(prep, 11)

                    def step(i, u):
                        v = 1 - u
                        if real(i - 2):
                            factors(i - 2, u)
                        if real(i):
                            x_bias(i, u)
                        if real(i + 2):
                            x_low(i + 2, u)
                        if real(i - 3):
                            scatter(i - 3, v)

                    schedule(po, step)
                    po.wait_ge(s_ready, NB)
                    po.wait_ge(slot_kept, NB)
                    for k in range(2):
                        po.wait_ge(scattered[k], 16 * J * NB // 2)

        with ExitStack() as c2:
            def sb2(name, shape, dt=F32):
                return c2.enter_context(nc.sbuf_tensor(name, shape, dt))

            def sem2(name):
                return c2.enter_context(nc.semaphore(name))

            wi_in = sb2("wi_in", [P, 2, I])
            wi_s = sb2("wi_s", [P, I])
            wiH = sb2("wiH", [P, 2, I], F32R)
            wiL = sb2("wiL", [P, 2, I], F32R)
            wo_in = sb2("wo_in", [P, 2, IC, D])
            woH = sb2("woH", [P, 2, IC, D], F32R)
            woL = sb2("woL", [P, 2, IC, D], F32R)
            hb = sb2("hb", [P, 2, IC])
            ob = sb2("ob", [P, 2])
            s_in = sb2("s_in", [P, 2, J, D])
            sH = sb2("sH", [P, 2, T], F32R)
            sL = sb2("sL", [P, 2, T], F32R)
            h = sb2("h", [P, IC, T])
            hH = sb2("hH", [P, 2, IC, T], F32R)
            hL = sb2("hL", [P, 2, IC, T], F32R)
            eT = sb2("eT", [P, T])
            e_out = sb2("e_out", [P, 2, J, D])

            wi_loaded = [sem2(f"wi_loaded{i}") for i in range(2)]
            wo_loaded = [sem2(f"wo_loaded{i}") for i in range(2)]
            s_loaded = [sem2(f"s_loaded{i}") for i in range(2)]
            e_stored = [sem2(f"e_stored{i}") for i in range(2)]
            ws_ready = sem2("ws_ready")
            wiH_ready = sem2("wiH_ready")
            wiL_ready = sem2("wiL_ready")
            woH_ready = sem2("woH_ready")
            woL_ready = sem2("woL_ready")
            ob_ready = sem2("ob_ready")
            hb_done = sem2("hb_done")
            hb_ready = sem2("hb_ready")
            sT_done = sem2("sT_done")
            sH_ready = sem2("sH_ready")
            sL_ready = sem2("sL_ready")
            in_done = sem2("in_done")
            h_ready = sem2("h_ready")
            hH_ready = sem2("hH_ready")
            hL_ready = sem2("hL_ready")
            down_done = sem2("down_done")
            eT_ready = sem2("eT_ready")
            back_done = sem2("back_done")
            e_ready = sem2("e_ready")
            NT = E * TPE
            slots_t = slots_dram.rearrange("(t p j) d -> p t (j d)", p=P, j=J)
            moe_t = moe_dram[0:S, :].rearrange("(t p j) d -> p t (j d)", p=P, j=J)
            inter_v = inter_w.rearrange("e d i -> d e i")
            output_v = output_w.rearrange("e (c p) d -> p e c d", p=P)

            def real(t):
                return not isinstance(t, int) or 0 <= t < NT

            def more(e):
                return not isinstance(e, int) or e < E

            def wait(eng, s, n):
                if not isinstance(n, int) or n > 0:
                    eng.wait_ge(s, n)

            def schedule(eng, step):
                for t in range(4):
                    step(t, t // 2, t)
                with eng.Fori(0, (NT - 8) // 4) as n:
                    for k in range(4):
                        step(n * 4 + (4 + k), n * 2 + (2 + k // 2), k)
                for t in range(NT - 4, NT + 2):
                    step(t, t // 2, t % 4)

            with nc.Block() as block:
                @block.sync
                def _(sp):
                    def weights(e, w):
                        wait(sp, ws_ready, e - 1)
                        wait(sp, hb_done, e - 1)
                        sp.dma_start(wi_in[:, w], inter_v[:, bass.ds(e, 1)]).then_inc(wi_loaded[w], 16)
                        wait(sp, woL_ready, e - 1)
                        sp.dma_start(wo_in[:, w:w + 1], output_v[:, bass.ds(e, 1)]).then_inc(wo_loaded[w], 16)

                    def tile(t, u):
                        wait(sp, sT_done, t - 1)
                        sp.dma_start(s_in[:, u].rearrange("p j d -> p (j d)"), slots_t[:, bass.ds(t, 1)])\
                            .then_inc(s_loaded[u], 16)

                    def store(t, u):
                        sp.wait_ge(e_ready, t + 1)
                        sp.dma_start(moe_t[:, bass.ds(t, 1)], e_out[:, u].rearrange("p j d -> p (j d)"))\
                            .then_inc(e_stored[u], 16)

                    tile(0, 0)
                    weights(0, 0)
                    tile(1, 1)
                    weights(1, 1)

                    def step(t, e, k):
                        if real(t + 2):
                            tile(t + 2, k % 2)
                        if k % 2 == 1 and more(e + 2):
                            weights(e + 2, k // 2)
                        if real(t - 2):
                            store(t - 2, k % 2)

                    schedule(sp, step)
                    for k in range(2):
                        sp.wait_ge(e_stored[k], 16 * NT // 2)

                @block.tensor
                def _(pe):
                    def turn(t, k):
                        pe.wait_ge(s_loaded[k % 2], (t // 2 + 1) * 16)
                        wait(pe, sL_ready, t)
                        for j in range(J):
                            mm = pe.transpose(psum[6][:, j * P:(j + 1) * P], s_in[:, k % 2, j], ident)
                        mm.then_inc(sT_done, 1)

                    def bias(e, w):
                        pe.wait_ge(wi_loaded[w], (e // 2 + 1) * 16)
                        wait(pe, hb_ready, e)
                        for c in range(IC):
                            mm = pe.matmul(psum[7][:, c:c + 1], wi_in[:, w, c * P:(c + 1) * P], vecs[:, 3:4],
                                           start=True, stop=True)
                        mm.then_inc(hb_done, 1)

                    def up(t, e, k, c):
                        w = k // 2
                        if c == 0:
                            pe.wait_ge(sL_ready, t + 1)
                            pe.wait_ge(wiL_ready, e + 1)
                        wait(pe, h_ready, IC * (t - 1) + c + 1)
                        q = slice(c * P, (c + 1) * P)
                        pe.matmul(psum[c][:], wiH[:, w, q], sH[:, k % 2], start=True, stop=False)
                        pe.matmul(psum[c][:], wiL[:, w, q], sH[:, k % 2], start=False, stop=False)
                        pe.matmul(psum[c][:], wiH[:, w, q], sL[:, k % 2], start=False, stop=True).then_inc(in_done, 1)

                    def down(t, e, k, c):
                        w = k // 2
                        if c == 0:
                            pe.wait_ge(woL_ready, e + 1)
                            wait(pe, eT_ready, t)
                        pe.wait_ge(hL_ready, IC * t + c + 1)
                        pe.matmul(psum[4][:], woH[:, w, c], hH[:, k % 2, c], start=(c == 0), stop=False)
                        pe.matmul(psum[4][:], woL[:, w, c], hH[:, k % 2, c], start=False, stop=False)
                        pe.matmul(psum[4][:], woH[:, w, c], hL[:, k % 2, c], start=False, stop=(c == IC - 1))\
                            .then_inc(down_done, 1)

                    def back(t):
                        pe.wait_ge(eT_ready, t + 1)
                        wait(pe, e_ready, t)
                        for j in range(J):
                            mm = pe.transpose(psum[5][:, j * P:(j + 1) * P], eT[:, j * P:(j + 1) * P], ident)
                        mm.then_inc(back_done, 1)

                    turn(0, 0)
                    bias(0, 0)

                    def step(t, e, k):
                        if real(t + 1):
                            turn(t + 1, (k + 1) % 4)
                        if k % 2 == 0 and more(e + 1):
                            bias(e + 1, 1 - k // 2)
                        for c in range(IC):
                            if real(t):
                                up(t, e, k, c)
                            if real(t - 1):
                                down(t - 1, e if k % 2 else e - 1, (k - 1) % 4, c)
                            if c == 1 and real(t - 2):
                                back(t - 2)

                    schedule(pe, step)

                @block.scalar
                def _(act):
                    def s_high(t, u):
                        act.wait_ge(sT_done, t + 1)
                        wait(act, in_done, IC * (t - 1))
                        act.activation(sH[:, u], psum[6][:], ACT.Copy).then_inc(sH_ready, 1)

                    def gelu(t, e, k, c):
                        act.wait_ge(in_done, IC * t + c + 1)
                        if c == 0:
                            act.wait_ge(hb_ready, e + 1)
                        wait(act, hL_ready, IC * (t - 1) + c + 1)
                        act.activation(h[:, c], psum[c][:], ACT.Gelu_apprx_tanh,
                                       bias=hb[:, k // 2, c:c + 1]).then_inc(h_ready, 1)

                    def e_bias(t, w):
                        act.wait_ge(down_done, IC * (t + 1))
                        wait(act, back_done, t)
                        act.activation(eT[:], psum[4][:], ACT.Identity, bias=ob[:, w:w + 1]).then_inc(eT_ready, 1)

                    def e_copy(t, u):
                        act.wait_ge(back_done, t + 1)
                        wait(act, e_stored[u], (t // 2) * 16)
                        act.activation(e_out[:, u].rearrange("p j d -> p (j d)"), psum[5][:], ACT.Copy)\
                            .then_inc(e_ready, 1)

                    s_high(0, 0)

                    def step(t, e, k):
                        if real(t + 1):
                            s_high(t + 1, 1 - k % 2)
                        if real(t):
                            gelu(t, e, k, 0)
                            gelu(t, e, k, 1)
                        if real(t - 2):
                            e_copy(t - 2, k % 2)
                        if real(t):
                            gelu(t, e, k, 2)
                            gelu(t, e, k, 3)
                        if real(t - 1):
                            e_bias(t - 1, (k - 1) % 4 // 2)

                    schedule(act, step)

                @block.gpsimd
                def _(po):
                    def split_out(e, w):
                        po.wait_ge(wo_loaded[w], (e // 2 + 1) * 16)
                        wait(po, down_done, IC * TPE * (e - 1))
                        po.tensor_tensor(woH[:, w], wo_in[:, w], zero_t[:, 0:I].rearrange("p (c d) -> p c d", c=IC), ALU.add).then_inc(woH_ready, 1)
                        po.wait_ge(woH_ready, e + 1)
                        po.tensor_tensor(woL[:, w], wo_in[:, w], woH[:, w].bitcast(F32), ALU.subtract)\
                            .then_inc(woL_ready, 1)

                    split_out(0, 0)
                    split_out(1, 1)
                    with po.Fori(0, (E - 2) // 2) as n:
                        split_out(n * 2 + 2, 0)
                        split_out(n * 2 + 3, 1)

                @block.vector
                def _(ve):
                    def prepare(e, w):
                        ve.wait_ge(wi_loaded[w], (e // 2 + 1) * 16)
                        wait(ve, wiL_ready, e)
                        ve.tensor_scalar(wi_s[:], wi_in[:, w], vecs[:, 2:3], None, ALU.mult).then_inc(ws_ready, 1)
                        ve.wait_ge(ws_ready, e + 1)
                        wait(ve, in_done, IC * TPE * (e - 1))
                        ve.tensor_copy(wiH[:, w], wi_s[:]).then_inc(wiH_ready, 1)
                        ve.wait_ge(wiH_ready, e + 1)
                        ve.tensor_tensor(wiL[:, w], wi_s[:], wiH[:, w].bitcast(F32), ALU.subtract).then_inc(wiL_ready, 1)
                        ve.wait_ge(hb_done, e + 1)
                        wait(ve, h_ready, IC * TPE * (e - 1))
                        ve.tensor_tensor(hb[:, w:w + 1], psum[7][:, 0:IC], e_bcol[:, bass.ds(e, 1)], ALU.add)\
                            .then_inc(hb_ready, 1)
                        wait(ve, eT_ready, TPE * (e - 1))
                        ve.tensor_copy(ob[:, w:w + 1], e_obcol[:, bass.ds(e, 1)]).then_inc(ob_ready, 1)

                    def s_low(t, u):
                        ve.wait_ge(sH_ready, t + 1)
                        wait(ve, in_done, IC * (t - 1))
                        ve.tensor_tensor(sL[:, u], psum[6][:], sH[:, u].bitcast(F32), ALU.subtract).then_inc(sL_ready, 1)

                    def h_split(t, u, c):
                        ve.wait_ge(h_ready, IC * t + c + 1)
                        wait(ve, down_done, IC * (t - 2) + c + 1)
                        ve.tensor_copy(hH[:, u, c], h[:, c]).then_inc(hH_ready, 1)
                        ve.wait_ge(hH_ready, IC * t + c + 1)
                        ve.tensor_tensor(hL[:, u, c], h[:, c], hH[:, u, c].bitcast(F32), ALU.subtract)\
                            .then_inc(hL_ready, 1)

                    ve.wait_ge(res_loaded, 64)
                    s_low(0, 0)
                    prepare(0, 0)

                    def step(t, e, k):
                        if real(t + 1):
                            s_low(t + 1, 1 - k % 2)
                        if real(t):
                            for c in range(IC):
                                h_split(t, k % 2, c)
                                if c == 1 and k % 2 == 0 and more(e + 1):
                                    prepare(e + 1, 1 - k // 2)

                    schedule(ve, step)
                    ve.wait_ge(ob_ready, E)

        with ExitStack() as c3:
            def sb3(name, shape, dt=F32):
                return c3.enter_context(nc.sbuf_tensor(name, shape, dt))

            def sem3(name):
                return c3.enter_context(nc.semaphore(name))

            xH = sb3("xH", [P, 2, T], F32R)
            xL = sb3("xL", [P, 2, T], F32R)
            h2 = sb3("h2", [P, 2, IC, T])
            rT = sb3("rT", [P, T])
            idx = sb3("idx", [P, 2, J], U32)
            coef = sb3("coef", [P, 2, J, 4])
            moe = sb3("moe", [P, 2, J, D])
            y0 = sb3("y0", [P, 2, J, D])
            y1 = sb3("y1", [P, J, D])
            y2 = sb3("y2", [P, 2, J, D])
            st2 = sb3("st2", [P, J, 6])
            mom2 = sb3("mom2", [P, J, 3])
            mean2 = sb3("mean2", [P, 2, J])
            var2 = sb3("var2", [P, J])
            ve2 = sb3("ve2", [P, 2, J])
            rs2 = sb3("rs2", [P, 2, J])
            res = sb3("res", [P, 2, J, D])

            xH_ready = sem3("xH_ready")
            xL_ready = sem3("xL_ready")
            in2_done = sem3("in2_done")
            h2_ready = sem3("h2_ready")
            out2_done = sem3("out2_done")
            rT_ready = sem3("rT_ready")
            back2_done = sem3("back2_done")
            idx_ready = sem3("idx_ready")
            coef_ready = sem3("coef_ready")
            gathered = [sem3(f"gathered{i}") for i in range(2)]
            y0_ready = sem3("y0_ready")
            y1_ready = sem3("y1_ready")
            y2_ready = sem3("y2_ready")
            st2_ready = sem3("st2_ready")
            mom2_step = sem3("mom2_step")
            mean2_ready = sem3("mean2_ready")
            ve2_ready = sem3("ve2_ready")
            rs2_ready = sem3("rs2_ready")
            res_ready = sem3("res_ready")
            stored = [sem3(f"stored{i}") for i in range(2)]
            out_v = out.rearrange("b (p j) d -> p b (j d)", j=J)

            def real(b):
                return not isinstance(b, int) or 0 <= b < NB

            def schedule(eng, step):
                for b in range(4):
                    step(b, b % 2)
                with eng.Fori(0, (NB - 6) // 2) as n:
                    step(n * 2 + 4, 0)
                    step(n * 2 + 5, 1)
                for b in range(NB - 2, NB + 3):
                    step(b, b % 2)

            with nc.Block() as block:
                @block.tensor
                def _(pe):
                    def up(b, u, c):
                        if c == 0:
                            pe.wait_ge(xL_ready, b + 1)
                        wait(pe, h2_ready, IC * (b - 1) + c + 1)
                        q = slice(c * P, (c + 1) * P)
                        pe.matmul(psum[c][:], resH[:, q], xH[:, u], start=True, stop=False)
                        pe.matmul(psum[c][:], resL[:, q], xH[:, u], start=False, stop=False)
                        pe.matmul(psum[c][:], resH[:, q], xL[:, u], start=False, stop=True).then_inc(in2_done, 1)

                    def down(b, u, c):
                        if c == 0:
                            wait(pe, rT_ready, b)
                        pe.wait_ge(h2_ready, IC * b + c + 1)
                        mm = pe.matmul(psum[4][:], res_out[:, c], h2[:, u, c], start=(c == 0), stop=(c == IC - 1))
                        if c == IC - 1:
                            mm.then_inc(out2_done, 1)

                    def back(b, u):
                        pe.wait_ge(rT_ready, b + 1)
                        wait(pe, y1_ready, J * (b - 1))
                        for j in range(J):
                            mm = pe.transpose(psum[5 + u][:, j * P:(j + 1) * P], rT[:, j * P:(j + 1) * P], ident)
                        mm.then_inc(back2_done, 1)

                    pe.wait_ge(res_loaded, 64)

                    def step(b, u):
                        for c in range(IC):
                            if real(b):
                                up(b, u, c)
                            if real(b - 1):
                                down(b - 1, 1 - u, c)
                            if c == 1 and real(b - 2):
                                back(b - 2, u)

                    schedule(pe, step)

                @block.scalar
                def _(act):
                    def x_high(b, u):
                        wait(act, in2_done, IC * (b - 1))
                        act.activation(xH[:, u:u + 1], kept[:, bass.ds(b, 1), 1], ACT.Copy).then_inc(xH_ready, 1)

                    act.wait_ge(res_loaded, 64)
                    x_high(0, 0)

                    def step(b, u):
                        if real(b + 1):
                            x_high(b + 1, 1 - u)
                        if real(b):
                            for c in range(IC):
                                act.wait_ge(in2_done, IC * b + c + 1)
                                wait(act, out2_done, b - 1)
                                act.activation(h2[:, u, c], psum[c][:], ACT.Gelu_apprx_tanh,
                                               bias=res_bias[:, c:c + 1]).then_inc(h2_ready, 1)
                        if real(b - 1):
                            act.wait_ge(out2_done, b)
                            wait(act, back2_done, b - 1)
                            act.activation(rT[:], psum[4][:], ACT.Identity, bias=res_obcol[:]).then_inc(rT_ready, 1)

                    schedule(act, step)

                @block.gpsimd
                def _(po):
                    def index(b, u):
                        wait(po, gathered[u], (b // 2) * 16 * J)
                        po.tensor_copy(idx[:, u:u + 1], slot_all[:, bass.ds(b, 1)]).then_inc(idx_ready, 1)

                    def weigh(b, u):
                        po.wait_ge(gathered[u], (b // 2 + 1) * 16 * J)
                        wait(po, y1_ready, J * (b - 1))
                        po.tensor_tensor(y0[:, u:u + 1], moe[:, u:u + 1],
                                         coef_all[:, bass.ds(b, 1), :, 2:3].broadcast_to([P, 1, J, D]),
                                         ALU.mult).then_inc(y0_ready, 1)

                    def coefs(b, u):
                        wait(po, y2_ready, J * (b - 1))
                        po.tensor_tensor(coef[:, u:u + 1], coef_all[:, bass.ds(b, 1)],
                                         coef_mul[:].rearrange("p (a j) n -> p a j n", a=1), ALU.mult)\
                            .then_inc(coef_ready, 1)

                    def gather(b, u):
                        for j in range(J):
                            po.indirect_dma_start(out=moe[:, u, j], out_offset=None, in_=moe_dram,
                                                  in_offset=bass.IndirectOffsetOnAxis(ap=idx[:, u, j:j + 1], axis=0),
                                                  bounds_check=S, oob_is_err=False).then_inc(gathered[u], 16)

                    def factor(b, u):
                        po.wait_ge(ve2_ready, b + 1)
                        wait(po, res_ready, J * (b - 1))
                        po.tensor_tensor(rs2[:, u], ve2[:, u], expo[:, 0:J], ALU.pow).then_inc(rs2_ready, 1)

                    index(0, 0)
                    index(1, 1)
                    po.wait_ge(idx_ready, 2)
                    gather(0, 0)
                    gather(1, 1)

                    def step(b, u):
                        v = 1 - u
                        if real(b - 1):
                            if real(b + 1):
                                index(b + 1, v)
                            weigh(b - 1, v)
                            if real(b + 1):
                                po.wait_ge(idx_ready, b + 2)
                                po.wait_ge(y0_ready, b)
                            coefs(b - 1, v)
                            if real(b + 1):
                                gather(b + 1, v)
                        if real(b - 2):
                            factor(b - 2, u)

                    schedule(po, step)

                @block.vector
                def _(ve):
                    def x_low(b, u):
                        ve.wait_ge(xH_ready, b + 1)
                        wait(ve, in2_done, IC * (b - 1))
                        ve.tensor_tensor(xL[:, u:u + 1], kept[:, bass.ds(b, 1), 1], xH[:, u:u + 1].bitcast(F32),
                                         ALU.subtract).then_inc(xL_ready, 1)

                    def total(b, u):
                        ve.wait_ge(back2_done, b + 1)
                        ve.wait_ge(y0_ready, b + 1)
                        ve.wait_ge(coef_ready, b + 1)
                        wait(ve, y2_ready, J * b)
                        for j in range(J):
                            ve.scalar_tensor_tensor(y1[:, j], psum[5 + u][:, j * D:(j + 1) * D], coef[:, u, j, 0:1],
                                                    y0[:, u, j], ALU.mult, ALU.add).then_inc(y1_ready, 1)
                        wait(ve, res_ready, J * (b - 1))
                        for j in range(J):
                            ve.wait_ge(y1_ready, J * b + j + 1)
                            ve.scalar_tensor_tensor(y2[:, u, j], kept[:, bass.ds(b, 1), 0, j * D:(j + 1) * D],
                                                    coef[:, u, j, 3:4], y1[:, j],
                                                    ALU.mult, ALU.add).then_inc(y2_ready, 1)
                        wait(ve, mean2_ready, b)
                        for j in range(J):
                            ve.wait_ge(y2_ready, J * b + j + 1)
                            ve.bn_stats(st2[:, j], y2[:, u, j]).then_inc(st2_ready, 1)
                        ve.wait_ge(st2_ready, J * (b + 1))
                        moments(ve, st2, mom2, var2, mom2_step, MS * b)
                        ve.tensor_scalar(mean2[:, u], mom2[:, :, 0], 0.5, None, ALU.mult).then_inc(mean2_ready, 1)
                        ve.wait_ge(mom2_step, MS * b + MS)
                        wait(ve, rs2_ready, b - 1)
                        ve.tensor_scalar(ve2[:, u], var2[:], LN_EPS, None, ALU.add).then_inc(ve2_ready, 1)

                    def norm(b, u):
                        ve.wait_ge(mean2_ready, b + 1)
                        ve.wait_ge(rs2_ready, b + 1)
                        wait(ve, stored[u], (b // 2) * 16)
                        for j in range(J):
                            ve.tensor_scalar(res[:, u, j], y2[:, u, j], mean2[:, u, j:j + 1], rs2[:, u, j:j + 1],
                                             ALU.subtract, ALU.mult).then_inc(res_ready, 1)

                    x_low(0, 0)

                    def step(b, u):
                        if real(b + 1):
                            x_low(b + 1, 1 - u)
                        if real(b - 3):
                            norm(b - 3, 1 - u)
                        if real(b - 2):
                            total(b - 2, u)

                    schedule(ve, step)

                @block.sync
                def _(sp):
                    def step(b, u):
                        if real(b - 3):
                            sp.wait_ge(res_ready, J * (b - 2))
                            sp.dma_start(out_v[:, bass.ds(b - 3, 1)], res[:, 1 - u].rearrange("p j d -> p (j d)"))\
                                .then_inc(stored[1 - u], 16)

                    schedule(sp, step)
                    for k in range(2):
                        sp.wait_ge(stored[k], 16 * NB // 2)


_OUT = (16, 512, 128)


def kernel(**inputs):
    import numpy as np
    import concourse.bacc as bacc
    from concourse.bass_utils import run_bass_kernel_spmd

    a = {k.removeprefix("L0_"): np.asarray(v) for k, v in inputs.items()}
    x = a["attn_x"]
    NB, T, D = x.shape
    P_, J = 128, T // 128
    E, _, I = a["ffn_inter_w"].shape
    w = a["attn_w_qkv"]
    c = np.ascontiguousarray
    consts = np.zeros((P_, 2 * P_ + J * E), np.float32)
    consts[:, :P_] = np.eye(P_)
    consts[:, P_:2 * P_] = np.triu(np.ones((P_, P_)), 1)
    consts[:, 2 * P_:] = np.tile(E - np.arange(E), J)
    arrays = {
        "x_tok": c(x),
        "x_T": c(x.reshape(NB, P_, J, D).transpose(3, 0, 2, 1).reshape(D, NB * T)),
        "wqT": c(w[:, :D].T), "wkT": c(w[:, D:2 * D].T), "wvT": c(w[:, 2 * D:].T),
        "w_proj": c(a["attn_w_proj"]),
        "b_q": c(a["attn_b_qkv"][:D]), "b_v": c(a["attn_b_qkv"][2 * D:]), "b_proj": c(a["attn_b_proj"]),
        "ln_w": c(a["ffn_attn_nw"]), "ln_b": c(a["ffn_attn_nb"]),
        "w_gate": c(a["ffn_wg"]), "w_coef": c(a["ffn_res_coef"]),
        "inter_w": c(a["ffn_inter_w"]),
        "inter_bT": c(a["ffn_inter_b"].reshape(E, I // P_, P_).transpose(2, 0, 1)),
        "output_w": c(a["ffn_output_w"]), "output_bT": c(a["ffn_output_b"].T),
        "res_w": c(a["ffn_res_inter_w"]), "res_bT": c(a["ffn_res_inter_b"].reshape(I // P_, P_).T),
        "res_out_w": c(a["ffn_res_output_w"]), "res_out_bT": c(a["ffn_res_output_b"].reshape(D, 1)),
        "consts": consts,
    }
    nc = bacc.Bacc("TRN2", target_bir_lowering=False, num_devices=1)
    args = {n: nc.dram_tensor(n, v.shape, mybir.dt.from_np(v.dtype), kind="ExternalInput").ap()
            for n, v in arrays.items()}
    out = nc.dram_tensor("out", _OUT, F32, kind="ExternalOutput").ap()
    build(nc, *args.values(), out)
    r = run_bass_kernel_spmd(nc, [arrays], core_ids=[0])
    return r.results[0]["out"]
```

```python
from contextlib import ExitStack

import concourse.bass as bass
from concourse import mybir

F32 = mybir.dt.float32
F32R = mybir.dt.float32r
BF16 = mybir.dt.bfloat16
U32 = mybir.dt.uint32
ALU = mybir.AluOpType
ACT = mybir.ActivationFunctionType
AX = mybir.AxisListType

P = 128
LN_EPS = 1e-5
GATE_LN_EPS = 1e-12


def build(nc, x_tok, x_T, w_attn, b_proj, small, inter_w, output_w, res_w, res_out_w, res_out_b, consts, out):
    NB, T, D = x_tok.shape
    J = T // P
    E, _, I = inter_w.shape
    IC = I // P
    S = NB * T
    CAP = max(4, -(-S // E))
    TPE = CAP // T
    NG = E + 2
    assert D == P and J == 4 and TPE == 2 and NB % 2 == 0

    slots_dram = nc.dram_tensor("slots_dram", [S, D], F32).ap()
    moe_dram = nc.dram_tensor("moe_dram", [S + 1, D], F32).ap()

    MS = 4

    def moments(ve, stats, mom, var, steps, done):
        ve.tensor_reduce(mom[:, :, 0:2], stats[:].rearrange("p j (h f) -> p j f h", h=2)[:, :, 1:3], AX.X, ALU.add)\
            .then_inc(steps, 1)
        ve.tensor_tensor(mom[:, :, 2], stats[:, :, 1], stats[:, :, 4], ALU.subtract).then_inc(steps, 1)
        ve.wait_ge(steps, done + 2)
        ve.scalar_tensor_tensor(var[:], mom[:, :, 2], 0.25, mom[:, :, 2], ALU.mult, ALU.mult).then_inc(steps, 1)
        ve.wait_ge(steps, done + 3)
        ve.scalar_tensor_tensor(var[:], mom[:, :, 1], 1.0 / D, var[:], ALU.mult, ALU.add).then_inc(steps, 1)

    with ExitStack() as ctx:
        def sb(name, shape, dt=F32):
            return ctx.enter_context(nc.sbuf_tensor(name, shape, dt))

        def sem(name):
            return ctx.enter_context(nc.semaphore(name))

        res_loaded = sem("res_loaded")
        vecs = sb("vecs", [P, 4 + NG + IC + E * IC + E])
        at = 4 + NG
        b_q, b_v, ln_w, ln_b = (vecs[:, n:n + 1] for n in range(4))
        gc_w = vecs[:, 4:at]
        res_bias = vecs[:, at:at + IC]
        e_bcol = vecs[:, at + IC:at + IC + E * IC].rearrange("p (e c) -> p e c", e=E)
        e_obcol = vecs[:, at + IC + E * IC:]
        bproj_row = sb("bproj_row", [1, D])
        cst = sb("cst", [P, 2 * P + J * E])
        ident_b = sb("ident_b", [P, P], BF16)
        upper_b = sb("upper_b", [P, P], BF16)
        ones_b = sb("ones_b", [P, P], BF16)
        ones_row = sb("ones_row", [2, P])
        ones_pair = sb("ones_pair", [2, P], F32R)
        bias_pair = sb("bias_pair", [2, D], F32R)
        bv_b = sb("bv_b", [P, P])
        expo = sb("expo", [P, 3 * J])
        aH = sb("aH", [P, D], F32R)
        aL = sb("aL", [P, D], F32R)
        c_z = sb("c_z", [P, 1])
        w_vp = sb("w_vp", [P, D])
        b_vp = sb("b_vp", [P, D])
        zero_t = sb("zero_t", [P, I])
        resH = sb("resH", [P, I], F32R)
        resL = sb("resL", [P, I], F32R)
        res_out = sb("res_out", [P, IC, D])
        ident = cst[:, 0:P]
        desc = cst[:, 2 * P:2 * P + J * E].rearrange("p (j e) -> p j e", j=J)

        kept = sb("kept", [P, NB, 2, T])
        slot_all = sb("slot_all", [P, NB, J], U32)
        coef_all = sb("coef_all", [P, NB, J, 4])

        psum = [ctx.enter_context(nc.psum_tensor(f"bank{i}", [P, 512], F32)) for i in range(8)]

        xn_both = sb("xn_both", [P, 2, 2, T])
        xn = xn_both[:, :, 0].rearrange("p u (j d) -> p u j d", j=J)
        xnT = xn_both[:, :, 1]
        slot_i = sb("slot_i", [P, 2, J], U32)
        slot_ready = sem("slot_ready")
        slot_kept = sem("slot_kept")
        scattered = [sem(f"scattered{i}") for i in range(2)]
        wi_in = sb("wi_in", [P, 2, I])
        wo_in = sb("wo_in", [P, 2, IC, D])
        s_in = sb("s_in", [P, 2, J, D])
        wi_loaded = [sem(f"wi_loaded{i}") for i in range(2)]
        wo_loaded = [sem(f"wo_loaded{i}") for i in range(2)]
        s_loaded = [sem(f"s_loaded{i}") for i in range(2)]
        wiL_ready = sem("wiL_ready")
        woL_ready = sem("woL_ready")
        sT_done = sem("sT_done")
        NT = E * TPE
        slots_t = slots_dram.rearrange("(t p j) d -> p t (j d)", p=P, j=J)
        inter_v = inter_w.rearrange("e d i -> d e i")
        output_v = output_w.rearrange("e (c p) d -> p e c d", p=P)
        e_out = sb("e_out", [P, 2, J, D])
        e_stored = [sem(f"e_stored{i}") for i in range(2)]
        xH = sb("xH", [P, 2, T], F32R)
        xL = sb("xL", [P, 2, T], F32R)
        h2 = sb("h2", [P, 2, IC, T])
        r_early = sb("r_early", [P, 2, T])
        xH_ready = sem("xH_ready")
        xL_ready = sem("xL_ready")
        in2_done = sem("in2_done")
        h2_ready = sem("h2_ready")
        out2_done = sem("out2_done")
        r_kept = sem("r_kept")
        y1_ready = sem("y1_ready")

        def wait(eng, s, n):
            if not isinstance(n, int) or n > 0:
                eng.wait_ge(s, n)

        EARLY = 2
        assert NB > 4 + EARLY and NB % 4 == 0

        def res_high(act, b, u):
            wait(act, in2_done, IC * (b - 1))
            act.activation(xH[:, u:u + 1], kept[:, bass.ds(b, 1), 1], ACT.Copy).then_inc(xH_ready, 1)

        def res_low(ve, b, u):
            ve.wait_ge(xH_ready, b + 1)
            wait(ve, in2_done, IC * (b - 1))
            ve.tensor_tensor(xL[:, u:u + 1], kept[:, bass.ds(b, 1), 1], xH[:, u:u + 1].bitcast(F32),
                             ALU.subtract).then_inc(xL_ready, 1)

        def res_up(pe, b, u, c):
            if c == 0:
                pe.wait_ge(xL_ready, b + 1)
            wait(pe, h2_ready, IC * (b - 1) + c + 1)
            q = slice(c * P, (c + 1) * P)
            pe.matmul(psum[c][:], resH[:, q], xH[:, u], start=True, stop=False)
            pe.matmul(psum[c][:], resL[:, q], xH[:, u], start=False, stop=False)
            pe.matmul(psum[c][:], resH[:, q], xL[:, u], start=False, stop=True).then_inc(in2_done, 1)

        def res_gelu(act, b, u, c):
            act.wait_ge(in2_done, IC * b + c + 1)
            wait(act, out2_done, b - 1)
            act.activation(h2[:, u, c], psum[c][:], ACT.Gelu_apprx_tanh, bias=res_bias[:, c:c + 1])\
                .then_inc(h2_ready, 1)

        def res_down(pe, b, u, k, j):
            if j == 0:
                if not isinstance(b, int) or b >= 4 + EARLY:
                    pe.wait_ge(y1_ready, J * (b - 3))
            R = psum[4 + k][:, j * D:(j + 1) * D]
            pe.matmul(R, ones_pair[:], bias_pair[:], start=True, stop=False)
            for c in range(IC):
                if j == 0:
                    pe.wait_ge(h2_ready, IC * b + c + 1)
                mm = pe.matmul(R, h2[:, u, c, j * P:(j + 1) * P], res_out[:, c], start=False, stop=(c == IC - 1))
            if j == J - 1:
                mm.then_inc(out2_done, 1)

        def res_keep(act, b):
            act.wait_ge(out2_done, b + 1)
            act.activation(r_early[:, b], psum[4 + b][:], ACT.Copy).then_inc(r_kept, 1)

        def load_weights(sp, e, w):
            wait(sp, wiL_ready, e - 1)
            sp.dma_start(wi_in[:, w], inter_v[:, bass.ds(e, 1)]).then_inc(wi_loaded[w], 16)
            wait(sp, woL_ready, e - 1)
            sp.dma_start(wo_in[:, w:w + 1], output_v[:, bass.ds(e, 1)]).then_inc(wo_loaded[w], 16)

        def load_tile(sp, t, u):
            wait(sp, sT_done, t - 1)
            sp.dma_start(s_in[:, u].rearrange("p j d -> p (j d)"), slots_t[:, bass.ds(t, 1)])\
                .then_inc(s_loaded[u], 16)

        def scatter(po, b, u):
            po.wait_ge(slot_ready, b + 1)
            po.tensor_copy(slot_all[:, bass.ds(b, 1)], slot_i[:, u:u + 1]).then_inc(slot_kept, 1)
            for j in range(J):
                po.indirect_dma_start(out=slots_dram,
                                      out_offset=bass.IndirectOffsetOnAxis(ap=slot_i[:, u, j:j + 1], axis=0),
                                      in_=xn[:, u, j], in_offset=None, bounds_check=S - 1,
                                      oob_is_err=False).then_inc(scattered[u], 16)

        with ExitStack() as c1:
            def sb1(name, shape, dt=F32):
                return c1.enter_context(nc.sbuf_tensor(name, shape, dt))

            def sem1(name):
                return c1.enter_context(nc.semaphore(name))

            bias_raw = sb1("bias_raw", [2, D])
            bias_hi = sb1("bias_hi", [2, D], F32R)
            bias_lo = sb1("bias_lo", [2, D])
            w_raw = sb1("w_raw", [P, 4, D])
            a_f = sb1("a_f", [P, D])
            res_raw = sb1("res_raw", [P, I])
            xt_in = sb1("xt_in", [P, 2, T])
            x_in = sb1("x_in", [P, 2, J, D])
            xtH = sb1("xtH", [P, 2, T], F32R)
            xtL = sb1("xtL", [P, 2, T], F32R)
            xb = sb1("xb", [P, 2, J, D])
            zH = sb1("zH", [P, 2, T], F32R)
            zL = sb1("zL", [P, 2, T], F32R)
            nmax = sb1("nmax", [P, 2, J])
            rsum = sb1("rsum", [P, 2, J])
            rinv = sb1("rinv", [P, J])
            prob = sb1("prob", [P, J, T])
            probT = sb1("probT", [P, 2, J, T])
            oT = sb1("oT", [P, T])
            r1 = sb1("r1", [P, 2, J, D])
            stats = sb1("stats", [P, J, 6])
            mom = sb1("mom", [P, J, 3])
            var = sb1("var", [P, J])
            vq = sb1("vq", [P, 2, 3, J])
            rs = sb1("rs", [P, 2, 3, J])
            nb = sb1("nb", [P, 2, J])
            lgd = sb1("lgd", [P, J, NG])
            gmx = sb1("gmx", [P, 2, J])
            cand = sb1("cand", [P, J, E])
            cm = sb1("cm", [P, 2, J])
            maskb = sb1("maskb", [P, 2, J, E], BF16)
            tsum = sb1("tsum", [P, 2, J, E], BF16)
            gex = sb1("gex", [P, 2, J, NG])
            gsum = sb1("gsum", [P, 2, J])
            grec = sb1("grec", [P, 2, J])
            cg = sb1("cg", [P, 2, J])
            lsel = sb1("lsel", [P, J, E])
            loc = sb1("loc", [P, J])
            slo = sb1("slo", [P, 2, J])

            w_loaded = sem1("w_loaded")
            zeroed = sem1("zeroed")
            zero_set = sem1("zero_set")
            prep = sem1("prep")
            prep_g = sem1("prep_g")
            prep_mm = sem1("prep_mm")
            prep_w = sem1("prep_w")
            consts_loaded = sem1("consts_loaded")
            res_w_loaded = sem1("res_w_loaded")
            xt_loaded = [sem1(f"xt_loaded{i}") for i in range(2)]
            x_loaded = [sem1(f"x_loaded{i}") for i in range(2)]
            xtH_ready = sem1("xtH_ready")
            xtL_ready = sem1("xtL_ready")
            xb_ready = sem1("xb_ready")
            z_done = sem1("z_done")
            zH_ready = sem1("zH_ready")
            zL_ready = sem1("zL_ready")
            scores_done = sem1("scores_done")
            max_ready = sem1("max_ready")
            prob_ready = sem1("prob_ready")
            t_done = sem1("t_done")
            probT_ready = sem1("probT_ready")
            pv_done = sem1("pv_done")
            oT_ready = sem1("oT_ready")
            proj_done = sem1("proj_done")
            rinv_ready = sem1("rinv_ready")
            r1_ready = sem1("r1_ready")
            stats_ready = sem1("stats_ready")
            mom_step = sem1("mom_step")
            vq_ready = sem1("vq_ready")
            rs_ready = sem1("rs_ready")
            nb_ready = sem1("nb_ready")
            s_ready = sem1("s_ready")
            xn_ready = sem1("xn_ready")
            xnT_done = sem1("xnT_done")
            xnT_ready = sem1("xnT_ready")
            xn_kept = [sem(f"xn_kept{i}") for i in range(2)]
            logit_done = sem1("logit_done")
            gate_step = sem1("gate_step")
            mask_ready = sem1("mask_ready")
            gex_ready = sem1("gex_ready")
            rank_done = sem1("rank_done")
            slot_step = sem1("slot_step")

            GS = 12
            SS = 5
            W_DMAS = 3
            LAST = 3

            def real(b):
                return not isinstance(b, int) or 0 <= b < NB

            def schedule(eng, step):
                for i in range(5):
                    step(i, i % 2)
                with eng.Fori(0, (NB - 8) // 2) as n:
                    step(n * 2 + 5, 1)
                    step(n * 2 + 6, 0)
                for i in range(NB - 3, NB + LAST):
                    step(i, i % 2)

            with nc.Block() as block:
                @block.sync
                def _(sp):
                    def load_xt(b, u):
                        wait(sp, xtL_ready, b - 1)
                        sp.dma_start(xt_in[:, u], x_T[:, bass.ds(b * T, T)]).then_inc(xt_loaded[u], 16)

                    def load_x(b, u):
                        wait(sp, xb_ready, b - 1)
                        wait(sp, pv_done, b - 1)
                        sp.dma_start(x_in[:, u].rearrange("p j d -> p (j d)"),
                                     x_tok.rearrange("b (p j) d -> p b (j d)", j=J)[:, bass.ds(b, 1)])\
                            .then_inc(x_loaded[u], 16)

                    sp.dma_start(w_raw[:].rearrange("p n d -> p (n d)"), w_attn).then_inc(w_loaded, 16)
                    load_xt(0, 0)
                    load_xt(1, 1)
                    load_x(0, 0)
                    sp.dma_start(res_raw[:], res_w).then_inc(res_w_loaded, 16)
                    sp.dma_start(bias_raw[:], res_out_b).then_inc(res_w_loaded, 16)
                    load_xt(2, 0)
                    slots_z = slots_dram.rearrange("(q p m r) d -> q p m (r d)", q=4, p=P, r=I // D)

                    def step(i, u):
                        v = 1 - u
                        if real(i + 3):
                            load_xt(i + 3, v)
                        if real(i + 1):
                            load_x(i + 1, v)
                        if real(i - 2):
                            sp.wait_ge(xnT_ready, i - 1)
                            sp.dma_start(kept[:, bass.ds(i - 2, 1)], xn_both[:, u]).then_inc(xn_kept[u], 16)
                        if isinstance(i, int) and i < 2:
                            sp.wait_ge(zero_set, 1)
                            for q in (2 * i, 2 * i + 1):
                                sp.dma_start(slots_z[q], zero_t[:].rearrange("p (a n) -> p a n", a=1)
                                             .broadcast_to([P, S // (4 * P * (I // D)), I])).then_inc(zeroed, 16)
                            if i == 1:
                                sp.dma_start(moe_dram[S:S + 1, :], zero_t[0:1, 0:D]).then_inc(zeroed, 16)

                    schedule(sp, step)
                    load_weights(sp, 0, 0)
                    load_weights(sp, 1, 1)
                    for k in range(2):
                        sp.wait_ge(xn_kept[k], 16 * NB // 2)
                    for k in range(2):
                        sp.wait_ge(scattered[k], 16 * J * NB // 2)
                    load_tile(sp, 0, 0)
                    load_tile(sp, 1, 1)

                @block.tensor
                def _(pe):
                    pe.wait_ge(w_loaded, 16 * W_DMAS)
                    pe.matmul(psum[0][:, 0:D], w_raw[:, 0], w_raw[:, 1], start=True, stop=True).then_inc(prep_mm, 1)
                    pe.matmul(psum[1][:, 0:1], w_raw[:, 1], b_q, start=True, stop=True).then_inc(prep_mm, 1)
                    pe.matmul(psum[2][:, 0:D], w_raw[:, 2], w_raw[:, 3], start=True, stop=True).then_inc(prep_mm, 1)
                    pe.wait_ge(prep, 2)
                    pe.wait_ge(prep_g, 4)
                    pe.matmul(psum[3][:, 0:D], bv_b[:], w_raw[:, 3], start=True, stop=False)
                    pe.matmul(psum[3][:, 0:D], ones_row[0:1, :], bproj_row[:], start=False, stop=True).then_inc(prep_mm, 1)

                    def scores(b, u):
                        pe.wait_ge(zL_ready, b + 1)
                        for j in range(J):
                            wait(pe, prob_ready, J * (b - 1) + j + 1)
                            q = slice(j * P, (j + 1) * P)
                            pe.matmul(psum[j][:], zH[:, u, q], xtH[:, u], start=True, stop=False)
                            pe.matmul(psum[j][:], zL[:, u, q], xtH[:, u], start=False, stop=False)
                            pe.matmul(psum[j][:], zH[:, u, q], xtL[:, u], start=False, stop=True)\
                                .then_inc(scores_done, 1)

                    def values(b, u, blocks):
                        if blocks[0] == 0:
                            pe.wait_ge(x_loaded[u], (b // 2 + 1) * 16)
                            pe.wait_ge(probT_ready, J * (b + 1))
                            wait(pe, r1_ready, J * b)
                        for k in blocks:
                            mm = pe.matmul(psum[6][:], x_in[:, u, k], probT[:, u, k], start=(k == 0), stop=(k == J - 1))
                        if blocks[-1] == J - 1:
                            mm.then_inc(pv_done, 1)

                    def rank(b, u):
                        pe.wait_ge(mask_ready, b + 1)
                        pe.wait_ge(gate_step, GS * b + 1)
                        R = psum[7][:, 0:J * E].rearrange("p (j e) -> p j e", j=J)
                        for k in range(J):
                            pe.matmul(R, upper_b[:], maskb[:, u, k:k + 1, :].broadcast_to([P, J, E]),
                                      start=(k == 0), stop=False, skip_group_check=True)
                            pe.matmul(R, ones_b[:], tsum[:, u, k:k + 1, :].broadcast_to([P, J, E]),
                                      start=False, stop=False, skip_group_check=True)
                        for k in range(J - 1):
                            mm = pe.matmul(R[:, k + 1:J], ident_b[:],
                                           maskb[:, u, k:k + 1, :].broadcast_to([P, J - 1 - k, E]),
                                           start=False, stop=(k == J - 2), skip_group_check=True)
                        mm.then_inc(rank_done, 1)

                    def project(b, u):
                        pe.wait_ge(xtL_ready, b + 1)
                        wait(pe, prob_ready, J * (b - 1) + 1)
                        pe.matmul(psum[0][:], aH[:], xtH[:, u], start=True, stop=False)
                        pe.matmul(psum[0][:], aL[:], xtH[:, u], start=False, stop=False)
                        pe.matmul(psum[0][:], aH[:], xtL[:, u], start=False, stop=True).then_inc(z_done, 1)

                    def turn_xn(b, u):
                        pe.wait_ge(xn_ready, J * (b + 1))
                        wait(pe, slot_step, SS * (b - 1) + 1)
                        for j in range(J):
                            mm = pe.transpose(psum[7][:, j * P:(j + 1) * P], xn[:, u, j], ident)
                        mm.then_inc(xnT_done, 1)

                    def turn_probs(b, u, blocks):
                        for j in blocks:
                            pe.wait_ge(prob_ready, J * b + j + 1)
                            wait(pe, probT_ready, J * b + j - 1)
                            for k in range(J):
                                mm = pe.transpose(psum[4 + j % 2][:, k * P:(k + 1) * P],
                                                  prob[:, j, k * P:(k + 1) * P], ident)
                            mm.then_inc(t_done, 1)

                    def out_proj(b, u):
                        pe.wait_ge(oT_ready, b + 1)
                        for j in range(J):
                            mm = pe.matmul(psum[6][:, j * D:(j + 1) * D], oT[:, j * P:(j + 1) * P], w_vp[:],
                                           start=True, stop=True)
                        mm.then_inc(proj_done, 1)

                    def logits(b, u):
                        pe.wait_ge(xnT_ready, b + 1)
                        for j in range(J):
                            mm = pe.matmul(psum[7][:, j * NG:(j + 1) * NG], xnT[:, u, j * P:(j + 1) * P], gc_w[:],
                                           start=True, stop=True)
                        mm.then_inc(logit_done, 1)

                    pe.wait_ge(prep, 5)
                    project(0, 0)
                    pe.wait_ge(prep, 10)
                    pe.wait_ge(consts_loaded, 16)

                    def step(i, u):
                        v = 1 - u
                        if real(i):
                            scores(i, u)
                        if real(i - 1):
                            values(i - 1, v, range(J - 1))
                        if real(i - 3):
                            rank(i - 3, v)
                        if real(i - 1):
                            values(i - 1, v, (J - 1,))
                        if isinstance(i, int) and i == NB + 1:
                            pe.wait_ge(res_loaded, 16)
                            pe.wait_ge(prep_w, 8)
                            pe.wait_ge(probT_ready, J * NB)
                            for c in range(IC):
                                res_down(pe, 0, 0, 0, c)
                        if real(i + 1):
                            project(i + 1, v)
                        if real(i - 2):
                            turn_xn(i - 2, u)
                        if isinstance(i, int) and i == NB + 1:
                            res_up(pe, 1, 1, 0)
                        if real(i - 1):
                            out_proj(i - 1, v)
                        if real(i):
                            turn_probs(i, u, (0, 1))
                        if real(i - 2):
                            logits(i - 2, u)
                        if real(i):
                            turn_probs(i, u, (2, 3))
                        if isinstance(i, int) and i == NB:
                            pe.wait_ge(prob_ready, J * NB)
                            for c in range(IC):
                                res_up(pe, 0, 0, c)
                        if isinstance(i, int) and i == NB + 1:
                            for c in range(1, IC - 1):
                                res_up(pe, 1, 1, c)

                    schedule(pe, step)
                    res_up(pe, 1, 1, IC - 1)
                    for c in range(IC):
                        res_down(pe, 1, 1, 1, c)

                @block.scalar
                def _(act):
                    act.dma_start(vecs[:], small).then_inc(w_loaded, 16)
                    act.dma_start(bproj_row[:], b_proj.rearrange("(a d) -> a d", a=1)).then_inc(w_loaded, 16)
                    act.dma_start(cst[:], consts).then_inc(consts_loaded, 16)
                    act.dma_start(res_out[:], res_out_w.rearrange("(c p) d -> p c d", p=P)).then_inc(res_loaded, 16)

                    def x_high(b, u):
                        act.wait_ge(xt_loaded[u], (b // 2 + 1) * 16)
                        wait(act, scores_done, J * (b - 1))
                        act.activation(xtH[:, u], xt_in[:, u], ACT.Copy).then_inc(xtH_ready, 1)

                    def z_high(b, u):
                        act.wait_ge(z_done, b + 1)
                        wait(act, scores_done, J * (b - 1))
                        act.activation(zH[:, u], psum[0][:], ACT.Identity, bias=c_z[:]).then_inc(zH_ready, 1)

                    def exps(b, u):
                        for j in range(J):
                            act.wait_ge(max_ready, J * b + j + 1)
                            wait(act, t_done, J * (b - 1) + j + 1)
                            if j == 0:
                                wait(act, rinv_ready, b - 1)
                            act.activation(prob[:, j], psum[j][:], ACT.Exp, bias=nmax[:, u, j:j + 1],
                                           accum_out=rsum[:, u, j:j + 1]).then_inc(prob_ready, 1)

                    def normalise(b, u):
                        act.wait_ge(nb_ready, b + 1)
                        wait(act, xnT_done, b - 1)
                        wait(act, xn_kept[u], (b // 2) * 16)
                        wait(act, scattered[u], (b // 2) * 16 * J)
                        for j in range(J):
                            act.activation(xn[:, u, j], r1[:, u, j], ACT.Identity, bias=nb[:, u, j:j + 1],
                                           scale=rs[:, u, 0, j:j + 1]).then_inc(xn_ready, 1)

                    def gate_exp(b, u):
                        act.wait_ge(gate_step, GS * b + 4)
                        wait(act, gate_step, GS * (b - 1))
                        act.activation(gex[:, u], lgd[:], ACT.Exp).then_inc(gex_ready, 1)

                    def o_copy(b, u):
                        act.wait_ge(pv_done, b + 1)
                        wait(act, proj_done, b)
                        act.activation(oT[:], psum[6][:], ACT.Copy).then_inc(oT_ready, 1)

                    def xnT_copy(b, u):
                        act.wait_ge(xnT_done, b + 1)
                        wait(act, logit_done, b - 1)
                        act.activation(xnT[:, u], psum[7][:], ACT.Identity, bias=ln_b, scale=ln_w).then_inc(xnT_ready, 1)

                    def probT_copy(b, u, j):
                        act.wait_ge(t_done, J * b + j + 1)
                        wait(act, pv_done, b - 1)
                        act.activation(probT[:, u, :, j * P:(j + 1) * P],
                                       psum[4 + j % 2][:].rearrange("p (k q) -> p k q", k=J), ACT.Copy)\
                            .then_inc(probT_ready, 1)

                    x_high(0, 0)
                    act.wait_ge(prep, 6)
                    z_high(0, 0)
                    x_high(1, 1)

                    def step(i, u):
                        v = 1 - u
                        if real(i):
                            exps(i, u)
                        if isinstance(i, int) and i == NB + 1:
                            normalise(i - 2, u)
                        if real(i - 3):
                            gate_exp(i - 3, v)
                        if real(i - 2) and not (isinstance(i, int) and i == NB + 1):
                            normalise(i - 2, u)
                        if real(i + 2):
                            x_high(i + 2, u)
                        if real(i - 1):
                            o_copy(i - 1, v)
                        if real(i + 1):
                            z_high(i + 1, v)
                        if real(i - 2):
                            xnT_copy(i - 2, u)
                        if real(i):
                            for j in range(J):
                                probT_copy(i, u, j)
                        if isinstance(i, int) and NB - 1 <= i < NB - 1 + EARLY:
                            act.wait_ge(xn_kept[i - (NB - 1)], 16)
                            res_high(act, i - (NB - 1), i - (NB - 1))
                        if isinstance(i, int) and i == NB:
                            for c in range(IC):
                                res_gelu(act, 0, 0, c)
                        if isinstance(i, int) and i == NB + 1:
                            res_keep(act, 0)

                    schedule(act, step)
                    for c in range(IC):
                        res_gelu(act, 1, 1, c)
                    res_keep(act, 1)

                @block.vector
                def _(ve):
                    ve.memset(ones_b[:], 1.0).then_inc(prep, 1)
                    ve.memset(ones_row[:], 1.0).then_inc(prep, 1)
                    ve.wait_ge(prep_mm, 1)
                    scale = float(D) ** -0.5
                    ve.tensor_scalar(a_f[:], psum[0][:, 0:D], scale, None, ALU.mult).then_inc(prep, 1)
                    ve.wait_ge(prep, 3)
                    ve.tensor_copy(aH[:], a_f[:]).then_inc(prep, 1)
                    ve.wait_ge(prep, 4)
                    ve.tensor_tensor(aL[:], a_f[:], aH[:].bitcast(F32), ALU.subtract).then_inc(prep, 1)
                    ve.wait_ge(prep_mm, 4)
                    ve.tensor_scalar(c_z[:], psum[1][:, 0:1], scale, None, ALU.mult).then_inc(prep, 1)
                    ve.tensor_copy(w_vp[:], psum[2][:, 0:D]).then_inc(prep, 1)
                    ve.tensor_copy(b_vp[:], psum[3][:, 0:D]).then_inc(prep, 1)
                    ve.wait_ge(consts_loaded, 16)
                    ve.tensor_copy(ident_b[:], ident).then_inc(prep, 1)
                    ve.tensor_copy(upper_b[:], cst[:, P:2 * P]).then_inc(prep, 1)
                    ve.memset(tsum[:, 0], 0.0).then_inc(prep_w, 1)
                    ve.wait_ge(prep_w, 1)
                    ve.wait_ge(prep, 6)

                    def z_low(b, u):
                        ve.wait_ge(zH_ready, b + 1)
                        wait(ve, scores_done, J * (b - 1))
                        ve.scalar_tensor_tensor(zL[:, u], psum[0][:], c_z[:], zH[:, u].bitcast(F32),
                                                ALU.add, ALU.subtract).then_inc(zL_ready, 1)

                    def row_max(b, u, j):
                        ve.wait_ge(scores_done, J * b + j + 1)
                        wait(ve, prob_ready, J * (b - 2) + j + 1)
                        ve.tensor_reduce(nmax[:, u, j:j + 1], psum[j][:], AX.X, ALU.max, negate=True)\
                            .then_inc(max_ready, 1)

                    def norm_bias(b, u):
                        ve.wait_ge(rs_ready, 2 * b + 1)
                        wait(ve, xn_ready, J * (b - 1))
                        ve.scalar_tensor_tensor(nb[:, u], mom[:, :, 0], -0.5, rs[:, u, 0], ALU.mult, ALU.mult)\
                            .then_inc(nb_ready, 1)

                    def slots_and_coefs(b, u):
                        s0, g0 = SS * b, GS * b
                        R = psum[7][:, 0:J * E].rearrange("p (j e) -> p j e", j=J)
                        ve.wait_ge(rank_done, b + 1)
                        wait(ve, slot_step, s0)
                        ve.tensor_tensor(lsel[:], R, maskb[:, u], ALU.mult).then_inc(slot_step, 1)
                        ve.wait_ge(gex_ready, b + 1)
                        ve.tensor_reduce(gsum[:, 0], gex[:, u, :, 0:E], AX.X, ALU.add).then_inc(gate_step, 1)
                        ve.wait_ge(slot_step, s0 + 1)
                        ve.tensor_reduce(loc[:], lsel[:], AX.X, ALU.add).then_inc(slot_step, 1)
                        ve.tensor_reduce(gsum[:, 1], gex[:, u, :, E:NG], AX.X, ALU.add).then_inc(gate_step, 1)
                        ve.wait_ge(slot_step, s0 + 2)
                        ve.scalar_tensor_tensor(slo[:, 0], cm[:, u], -float(CAP), loc[:], ALU.mult, ALU.add)\
                            .then_inc(slot_step, 1)
                        ve.wait_ge(gate_step, g0 + 9)
                        ve.reciprocal(grec[:], gsum[:]).then_inc(gate_step, 1)
                        ve.wait_ge(slot_step, s0 + 3)
                        ve.scalar_tensor_tensor(slo[:, 1], loc[:], float(CAP), slo[:, 0], ALU.is_lt, ALU.mult)\
                            .then_inc(slot_step, 1)
                        ve.wait_ge(gate_step, g0 + 10)
                        ve.tensor_tensor(coef_all[:, bass.ds(b, 1), :, 0:2], gex[:, u, :, E:NG], spread(grec[:, 1], 2),
                                         ALU.mult).then_inc(gate_step, 1)
                        ve.wait_ge(slot_step, s0 + 4)
                        wait(ve, scattered[u], (b // 2) * 16 * J)
                        wait(ve, slot_kept, b - 1)
                        ve.tensor_scalar(slot_i[:, u], slo[:, 1], float(S), None, ALU.add).then_inc(slot_ready, 1)
                        ve.wait_ge(gate_step, g0 + 11)
                        ve.tensor_tensor(cg[:, u], coefs(b, 1), grec[:, 0], ALU.mult).then_inc(gate_step, 1)

                    def slot_coef(b, u):
                        ve.wait_ge(gate_step, GS * (b + 1))
                        ve.scalar_tensor_tensor(coefs(b, 2), loc[:], float(CAP), cg[:, u], ALU.is_lt, ALU.mult)\
                            .then_inc(slot_step, 1)

                    def row_sums(b, u):
                        ve.wait_ge(prob_ready, J * (b + 1))
                        wait(ve, r1_ready, J * b)
                        ve.reciprocal(rinv[:], rsum[:, u]).then_inc(rinv_ready, 1)

                    def x_norm(b, u):
                        ve.wait_ge(rinv_ready, b + 1)
                        ve.wait_ge(proj_done, b + 1)
                        ve.wait_ge(xb_ready, b + 1)
                        wait(ve, xn_ready, J * (b - 1))
                        for j in range(J):
                            ve.scalar_tensor_tensor(r1[:, u, j], psum[6][:, j * D:(j + 1) * D], rinv[:, j:j + 1],
                                                    xb[:, u, j], ALU.mult, ALU.add).then_inc(r1_ready, 1)
                        wait(ve, mom_step, MS * b)
                        for j in range(J):
                            ve.wait_ge(r1_ready, J * b + j + 1)
                            ve.bn_stats(stats[:, j], r1[:, u, j]).then_inc(stats_ready, 1)
                        ve.wait_ge(stats_ready, J * (b + 1))
                        wait(ve, nb_ready, b)
                        moments(ve, stats, mom, var, mom_step, MS * b)
                        ve.wait_ge(mom_step, MS * b + MS)
                        wait(ve, s_ready, b - 1)
                        ve.tensor_scalar(vq[:, u, 0:2],
                                         var[:].rearrange("p (a j) -> p a j", a=1).broadcast_to([P, 2, J]),
                                         1.0 + GATE_LN_EPS, GATE_LN_EPS * LN_EPS, ALU.mult, ALU.add)\
                            .then_inc(vq_ready, 1)
                        ve.tensor_scalar(vq[:, u, 2], var[:], LN_EPS, None, ALU.add).then_inc(vq_ready, 1)

                    def coefs(b, n):
                        return coef_all[:, bass.ds(b, 1), :, n]

                    def spread(t, n):
                        return t.rearrange("p (j a) -> p j a", a=1).broadcast_to([P, J, n])

                    def gate(b, u):
                        g0 = GS * b

                        def after(n):
                            ve.wait_ge(gate_step, g0 + n)

                        L = psum[7][:, 0:J * NG].rearrange("p (j e) -> p j e", j=J)
                        ve.wait_ge(logit_done, b + 1)
                        wait(ve, gate_step, g0)
                        ve.tensor_reduce(gmx[:, 0], L[:, :, 0:E], AX.X, ALU.max).then_inc(gate_step, 1)
                        ve.tensor_reduce(gmx[:, 1], L[:, :, E:NG], AX.X, ALU.max).then_inc(gate_step, 1)
                        after(1)
                        wait(ve, gex_ready, b)
                        ve.tensor_tensor(lgd[:, :, 0:E], L[:, :, 0:E], spread(gmx[:, 0], E), ALU.subtract)\
                            .then_inc(gate_step, 1)
                        after(2)
                        ve.tensor_tensor(lgd[:, :, E:NG], L[:, :, E:NG], spread(gmx[:, 1], 2), ALU.subtract)\
                            .then_inc(gate_step, 1)
                        after(3)
                        ve.scalar_tensor_tensor(cand[:], lgd[:, :, 0:E], 0.0, desc, ALU.is_ge, ALU.mult)\
                            .then_inc(gate_step, 1)
                        after(5)
                        wait(ve, slot_step, SS * (b - 1))
                        ve.tensor_reduce(cm[:, u], cand[:], AX.X, ALU.max).then_inc(gate_step, 1)
                        after(6)
                        wait(ve, rank_done, b - 1)
                        ve.tensor_tensor(maskb[:, u], desc, spread(cm[:, u], E), ALU.is_equal)\
                            .then_inc(mask_ready, 1)
                        ve.wait_ge(mask_ready, b + 1)
                        wait(ve, rank_done, b)
                        ve.tensor_tensor(tsum[:, 1 - u], tsum[:, u], maskb[:, u], ALU.add).then_inc(gate_step, 1)

                    z_low(0, 0)
                    ve.wait_ge(res_w_loaded, 32)
                    ve.tensor_copy(resH[:], res_raw[:]).then_inc(prep_w, 1)
                    ve.wait_ge(prep_w, 2)
                    ve.tensor_tensor(resL[:], res_raw[:], resH[:].bitcast(F32), ALU.subtract).then_inc(prep_w, 1)
                    ve.tensor_copy(bias_hi[:], bias_raw[:]).then_inc(prep_w, 1)
                    ve.wait_ge(prep_w, 4)
                    ve.tensor_tensor(bias_lo[:], bias_raw[:], bias_hi[:].bitcast(F32), ALU.subtract).then_inc(prep_w, 1)
                    ve.wait_ge(prep_w, 5)
                    ve.tensor_scalar(bias_lo[:], bias_lo[:], cst[0:2, 1:2], None, ALU.mult).then_inc(prep_w, 1)
                    ve.wait_ge(prep_w, 6)
                    ve.scalar_tensor_tensor(bias_pair[:], bias_hi[:].bitcast(F32), cst[0:2, 0:1], bias_lo[:],
                                            ALU.mult, ALU.add).then_inc(prep_w, 1)
                    ve.tensor_copy(ones_pair[:], ones_row[:]).then_inc(prep_w, 1)

                    def step(i, u):
                        v = 1 - u
                        if real(i):
                            row_max(i, u, 0)
                            row_max(i, u, 1)
                        if real(i - 2):
                            norm_bias(i - 2, u)
                        if real(i):
                            row_max(i, u, 2)
                            row_max(i, u, 3)
                        if real(i - 3):
                            gate(i - 3, v)
                            slots_and_coefs(i - 3, v)
                        if real(i - 1):
                            row_sums(i - 1, v)
                        if real(i + 1):
                            z_low(i + 1, v)
                        if real(i - 3):
                            slot_coef(i - 3, v)
                        if real(i - 1):
                            x_norm(i - 1, v)
                        if isinstance(i, int) and NB - 1 <= i < NB - 1 + EARLY:
                            ve.wait_ge(xn_kept[i - (NB - 1)], 16)
                            res_low(ve, i - (NB - 1), i - (NB - 1))

                    schedule(ve, step)
                    ve.wait_ge(slot_step, SS * NB)
                    ve.wait_ge(gate_step, GS * NB)

                @block.gpsimd
                def _(po):
                    po.memset(zero_t[:], 0.0).then_inc(zero_set, 1)
                    po.memset(expo[:, 0:J], -0.5).then_inc(prep_g, 1)
                    po.memset(expo[:, J:2 * J], 0.5).then_inc(prep_g, 1)
                    po.memset(expo[:, 2 * J:3 * J], -0.5).then_inc(prep_g, 1)
                    po.wait_ge(w_loaded, 16 * W_DMAS)
                    po.tensor_copy(bv_b[:], b_v.broadcast_to([P, P])).then_inc(prep_g, 1)
                    po.wait_ge(prep_g, 4)

                    def x_low(b, u):
                        po.wait_ge(xtH_ready, b + 1)
                        wait(po, scores_done, J * (b - 1))
                        po.tensor_tensor(xtL[:, u], xt_in[:, u], xtH[:, u].bitcast(F32), ALU.subtract)\
                            .then_inc(xtL_ready, 1)

                    def x_bias(b, u):
                        po.wait_ge(x_loaded[u], (b // 2 + 1) * 16)
                        wait(po, r1_ready, J * (b - 1))
                        po.tensor_tensor(xb[:, u], x_in[:, u],
                                         b_vp[:].rearrange("p (a d) -> p a d", a=1).broadcast_to([P, J, D]),
                                         ALU.add).then_inc(xb_ready, 1)

                    def factors(b, u):
                        po.wait_ge(vq_ready, 2 * b + 2)
                        wait(po, xn_ready, J * (b - 1))
                        po.tensor_tensor(rs[:, u, 0], vq[:, u, 0], expo[:, 0:J], ALU.pow).then_inc(rs_ready, 1)
                        wait(po, s_ready, b - 1)
                        po.tensor_tensor(rs[:, u, 1:3], vq[:, u, 1:3],
                                         expo[:, J:3 * J].rearrange("p (a j) -> p a j", a=2), ALU.pow)\
                            .then_inc(rs_ready, 1)
                        po.wait_ge(rs_ready, 2 * b + 2)
                        po.tensor_tensor(coef_all[:, bass.ds(b, 1), :, 3], rs[:, u, 1], rs[:, u, 2], ALU.mult)\
                            .then_inc(s_ready, 1)

                    x_low(0, 0)
                    x_low(1, 1)
                    po.wait_ge(prep, 8)

                    def step(i, u):
                        v = 1 - u
                        if real(i - 2):
                            factors(i - 2, u)
                        if real(i):
                            x_bias(i, u)
                        if real(i + 2):
                            x_low(i + 2, u)
                        if real(i - 3):
                            if isinstance(i, int) and i == 3:
                                po.wait_ge(zeroed, 80)
                            scatter(po, i - 3, v)

                    schedule(po, step)
                    po.wait_ge(s_ready, NB)
                    po.wait_ge(slot_kept, NB)

        with ExitStack() as c2:
            def sb2(name, shape, dt=F32):
                return c2.enter_context(nc.sbuf_tensor(name, shape, dt))

            def sem2(name):
                return c2.enter_context(nc.semaphore(name))

            wiH = sb2("wiH", [P, 2, I], F32R)
            wiL = sb2("wiL", [P, 2, I], F32R)
            woH = sb2("woH", [P, 2, IC, D], F32R)
            woL = sb2("woL", [P, 2, IC, D], F32R)
            hb = sb2("hb", [P, 2, IC])
            s_f = sb2("s_f", [P, T])
            ob = sb2("ob", [P, 2])
            sH = sb2("sH", [P, 2, T], F32R)
            sL = sb2("sL", [P, 2, T], F32R)
            h = sb2("h", [P, IC, T])
            hH = sb2("hH", [P, 2, IC, T], F32R)
            hL = sb2("hL", [P, 2, IC, T], F32R)
            eT = sb2("eT", [P, T])

            wiH_ready = sem2("wiH_ready")
            woH_ready = sem2("woH_ready")
            ob_ready = sem2("ob_ready")
            sT_ready = sem2("sT_ready")
            hb_ready = sem2("hb_ready")
            sH_ready = sem2("sH_ready")
            sL_ready = sem2("sL_ready")
            in_done = sem2("in_done")
            h_ready = sem2("h_ready")
            hH_ready = sem2("hH_ready")
            hL_ready = sem2("hL_ready")
            down_done = sem2("down_done")
            eT_ready = sem2("eT_ready")
            back_done = sem2("back_done")
            e_ready = sem2("e_ready")
            moe_t = moe_dram[0:S, :].rearrange("(t p j) d -> p t (j d)", p=P, j=J)

            def real(t):
                return not isinstance(t, int) or 0 <= t < NT

            def more(e):
                return not isinstance(e, int) or e < E

            def schedule(eng, step):
                for t in range(4):
                    step(t, t // 2, t)
                with eng.Fori(0, (NT - 8) // 4) as n:
                    for k in range(4):
                        step(n * 4 + (4 + k), n * 2 + (2 + k // 2), k)
                for t in range(NT - 4, NT + 2):
                    step(t, t // 2, t % 4)

            with nc.Block() as block:
                @block.sync
                def _(sp):
                    def store(t, u):
                        sp.wait_ge(e_ready, t + 1)
                        sp.dma_start(moe_t[:, bass.ds(t, 1)], e_out[:, u].rearrange("p j d -> p (j d)"))\
                            .then_inc(e_stored[u], 16)


                    def step(t, e, k):
                        if real(t + 2):
                            load_tile(sp, t + 2, k % 2)
                        if k % 2 == 1 and more(e + 2):
                            load_weights(sp, e + 2, k // 2)
                        if real(t - 2):
                            store(t - 2, k % 2)

                    schedule(sp, step)

                @block.tensor
                def _(pe):
                    def turn(t, k):
                        pe.wait_ge(s_loaded[k % 2], (t // 2 + 1) * 16)
                        wait(pe, sT_ready, t)
                        for j in range(J):
                            mm = pe.transpose(psum[6][:, j * P:(j + 1) * P], s_in[:, k % 2, j], ident)
                        mm.then_inc(sT_done, 1)

                    def up(t, e, k, c):
                        w = k // 2
                        if c == 0:
                            pe.wait_ge(sL_ready, t + 1)
                            pe.wait_ge(wiL_ready, e + 1)
                        wait(pe, h_ready, IC * (t - 1) + c + 1)
                        q = slice(c * P, (c + 1) * P)
                        pe.matmul(psum[c][:], wiH[:, w, q], sH[:, k % 2], start=True, stop=False)
                        pe.matmul(psum[c][:], wiL[:, w, q], sH[:, k % 2], start=False, stop=False)
                        pe.matmul(psum[c][:], wiH[:, w, q], sL[:, k % 2], start=False, stop=True).then_inc(in_done, 1)

                    def down(t, e, k, c):
                        w = k // 2
                        if c == 0:
                            pe.wait_ge(woL_ready, e + 1)
                            wait(pe, eT_ready, t)
                        pe.wait_ge(hL_ready, IC * t + c + 1)
                        pe.matmul(psum[4][:], woH[:, w, c], hH[:, k % 2, c], start=(c == 0), stop=False)
                        pe.matmul(psum[4][:], woL[:, w, c], hH[:, k % 2, c], start=False, stop=False)
                        pe.matmul(psum[4][:], woH[:, w, c], hL[:, k % 2, c], start=False, stop=(c == IC - 1))\
                            .then_inc(down_done, 1)

                    def back(t):
                        pe.wait_ge(eT_ready, t + 1)
                        wait(pe, e_ready, t)
                        for j in range(J):
                            mm = pe.transpose(psum[5][:, j * P:(j + 1) * P], eT[:, j * P:(j + 1) * P], ident)
                        mm.then_inc(back_done, 1)

                    turn(0, 0)

                    def step(t, e, k):
                        if real(t + 1):
                            turn(t + 1, (k + 1) % 4)
                        for c in range(IC):
                            if real(t):
                                up(t, e, k, c)
                            if isinstance(t, int) and t == NT:
                                pe.wait_ge(h_ready, IC * (NT - 1) + c + 1)
                                res_up(pe, EARLY, EARLY % 2, c)
                            if real(t - 1):
                                down(t - 1, e if k % 2 else e - 1, (k - 1) % 4, c)
                            if c == 1 and real(t - 2):
                                back(t - 2)

                    schedule(pe, step)

                @block.scalar
                def _(act):
                    def s_norm(t, u):
                        act.wait_ge(sT_done, t + 1)
                        wait(act, sL_ready, t)
                        act.activation(s_f[:], psum[6][:], ACT.Identity, bias=ln_b, scale=ln_w).then_inc(sT_ready, 1)

                    def gelu(t, e, k, c):
                        act.wait_ge(in_done, IC * t + c + 1)
                        if c == 0:
                            act.wait_ge(hb_ready, e + 1)
                        wait(act, hL_ready, IC * (t - 1) + c + 1)
                        act.activation(h[:, c], psum[c][:], ACT.Gelu_apprx_tanh,
                                       bias=hb[:, k // 2, c:c + 1]).then_inc(h_ready, 1)

                    def e_bias(t, w):
                        act.wait_ge(down_done, IC * (t + 1))
                        wait(act, back_done, t)
                        act.activation(eT[:], psum[4][:], ACT.Identity, bias=ob[:, w:w + 1]).then_inc(eT_ready, 1)

                    def e_copy(t, u):
                        act.wait_ge(back_done, t + 1)
                        wait(act, e_stored[u], (t // 2) * 16)
                        act.activation(e_out[:, u].rearrange("p j d -> p (j d)"), psum[5][:], ACT.Copy)\
                            .then_inc(e_ready, 1)

                    s_norm(0, 0)

                    def step(t, e, k):
                        if real(t + 1):
                            s_norm(t + 1, 1 - k % 2)
                        if isinstance(t, int) and t == NT - 1:
                            res_high(act, EARLY, EARLY % 2)
                        if real(t):
                            gelu(t, e, k, 0)
                            gelu(t, e, k, 1)
                        if isinstance(t, int) and t == NT:
                            for c in range(2):
                                res_gelu(act, EARLY, EARLY % 2, c)
                        if real(t - 2):
                            e_copy(t - 2, k % 2)
                        if real(t):
                            gelu(t, e, k, 2)
                            gelu(t, e, k, 3)
                        if isinstance(t, int) and t == NT:
                            res_high(act, EARLY + 1, (EARLY + 1) % 2)
                            for c in range(2, IC):
                                res_gelu(act, EARLY, EARLY % 2, c)
                        if real(t - 1):
                            e_bias(t - 1, (k - 1) % 4 // 2)

                    schedule(act, step)

                @block.gpsimd
                def _(po):
                    def split_out(e, w):
                        po.wait_ge(wo_loaded[w], (e // 2 + 1) * 16)
                        wait(po, down_done, IC * TPE * (e - 1))
                        po.tensor_tensor(woH[:, w], wo_in[:, w], zero_t[:, 0:I].rearrange("p (c d) -> p c d", c=IC), ALU.add).then_inc(woH_ready, 1)
                        po.wait_ge(woH_ready, e + 1)
                        po.tensor_tensor(woL[:, w], wo_in[:, w], woH[:, w].bitcast(F32), ALU.subtract)\
                            .then_inc(woL_ready, 1)

                    split_out(0, 0)
                    split_out(1, 1)
                    with po.Fori(0, (E - 2) // 2) as n:
                        split_out(n * 2 + 2, 0)
                        split_out(n * 2 + 3, 1)

                @block.vector
                def _(ve):
                    def prepare(e, w):
                        ve.wait_ge(wi_loaded[w], (e // 2 + 1) * 16)
                        wait(ve, in_done, IC * TPE * (e - 1))
                        ve.tensor_copy(wiH[:, w], wi_in[:, w]).then_inc(wiH_ready, 1)
                        ve.wait_ge(wiH_ready, e + 1)
                        ve.tensor_tensor(wiL[:, w], wi_in[:, w], wiH[:, w].bitcast(F32), ALU.subtract)\
                            .then_inc(wiL_ready, 1)
                        wait(ve, h_ready, IC * TPE * (e - 1))
                        ve.tensor_copy(hb[:, w:w + 1], e_bcol[:, bass.ds(e, 1)]).then_inc(hb_ready, 1)
                        wait(ve, eT_ready, TPE * (e - 1))
                        ve.tensor_copy(ob[:, w:w + 1], e_obcol[:, bass.ds(e, 1)]).then_inc(ob_ready, 1)

                    def s_split(t, u):
                        ve.wait_ge(sT_ready, t + 1)
                        wait(ve, in_done, IC * (t - 1))
                        ve.tensor_copy(sH[:, u], s_f[:]).then_inc(sH_ready, 1)
                        ve.wait_ge(sH_ready, t + 1)
                        ve.tensor_tensor(sL[:, u], s_f[:], sH[:, u].bitcast(F32), ALU.subtract).then_inc(sL_ready, 1)

                    def h_split(t, u, c):
                        ve.wait_ge(h_ready, IC * t + c + 1)
                        wait(ve, down_done, IC * (t - 2) + c + 1)
                        ve.tensor_copy(hH[:, u, c], h[:, c]).then_inc(hH_ready, 1)
                        ve.wait_ge(hH_ready, IC * t + c + 1)
                        ve.tensor_tensor(hL[:, u, c], h[:, c], hH[:, u, c].bitcast(F32), ALU.subtract)\
                            .then_inc(hL_ready, 1)

                    prepare(0, 0)
                    s_split(0, 0)

                    def step(t, e, k):
                        if real(t + 1):
                            s_split(t + 1, 1 - k % 2)
                        if isinstance(t, int) and NT - 1 <= t <= NT:
                            res_low(ve, EARLY + t - (NT - 1), (EARLY + t - (NT - 1)) % 2)
                        if real(t):
                            for c in range(IC):
                                h_split(t, k % 2, c)
                                if c == 1 and k % 2 == 0 and more(e + 1):
                                    prepare(e + 1, 1 - k // 2)

                    schedule(ve, step)
                    ve.wait_ge(ob_ready, E)

        with ExitStack() as c3:
            def sb3(name, shape, dt=F32):
                return c3.enter_context(nc.sbuf_tensor(name, shape, dt))

            def sem3(name):
                return c3.enter_context(nc.semaphore(name))

            idx = sb3("idx", [P, 4, J], U32)
            coef = sb3("coef", [P, 4, J, 4])
            moe = sb3("moe", [P, 4, J, D])
            y0 = sb3("y0", [P, 2, J, D])
            y1 = sb3("y1", [P, J, D])
            y2 = sb3("y2", [P, 2, J, D])
            st2 = sb3("st2", [P, J, 6])
            mom2 = sb3("mom2", [P, J, 3])
            mean2 = sb3("mean2", [P, 2, J])
            var2 = sb3("var2", [P, J])
            ve2 = sb3("ve2", [P, 2, J])
            rs2 = sb3("rs2", [P, 2, J])
            res = sb3("res", [P, 2, J, D])

            idx_ready = sem3("idx_ready")
            coef_ready = sem3("coef_ready")
            gathered = [sem3(f"gathered{i}") for i in range(4)]
            y0_ready = sem3("y0_ready")
            y2_ready = sem3("y2_ready")
            st2_ready = sem3("st2_ready")
            mom2_step = sem3("mom2_step")
            mean2_ready = sem3("mean2_ready")
            ve2_ready = sem3("ve2_ready")
            rs2_ready = sem3("rs2_ready")
            res_ready = sem3("res_ready")
            stored = [sem3(f"stored{i}") for i in range(2)]
            out_v = out.rearrange("b (p j) d -> p b (j d)", j=J)

            def real(b):
                return not isinstance(b, int) or 0 <= b < NB

            def late(b, first=EARLY):
                return not isinstance(b, int) or first <= b < NB

            def schedule(eng, step):
                for b in range(EARLY, 6):
                    step(b, b % 2, b % 4)
                with eng.Fori(0, (NB - 8) // 4) as n:
                    for m in range(4):
                        step(n * 4 + (6 + m), m % 2, (6 + m) % 4)
                for b in range(NB - 2, NB + 3):
                    step(b, b % 2, b % 4)

            with nc.Block() as block:
                @block.tensor
                def _(pe):
                    def step(b, u, k):
                        for c in range(IC):
                            if late(b, EARLY + 1):
                                res_up(pe, b, u, c)
                            if late(b - 1):
                                res_down(pe, b - 1, 1 - u, (k - 1) % 4, c)

                    schedule(pe, step)

                @block.scalar
                def _(act):
                    def coefs(b, k):
                        wait(act, y2_ready, J * (b - 3))
                        act.activation(coef[:, k:k + 1, :, 0:3], coef_all[:, bass.ds(b, 1), :, 0:3], ACT.Copy)\
                            .then_inc(coef_ready, 1)
                        act.activation(coef[:, k:k + 1, :, 3], coef_all[:, bass.ds(b, 1), :, 3], ACT.Copy, scale=2.0)\
                            .then_inc(coef_ready, 1)

                    def weigh(b, u, k):
                        act.wait_ge(coef_ready, 2 * b + 2)
                        act.wait_ge(gathered[k], (b // 4 + 1) * 16 * J)
                        wait(act, y1_ready, J * (b - 1))
                        for j in range(J):
                            act.activation(y0[:, u, j], moe[:, k, j], ACT.Copy, scale=coef[:, k, j, 2:3])\
                                .then_inc(y0_ready, 1)

                    for b in range(EARLY):
                        coefs(b, b)

                    def step(b, u, k):
                        if real(b - 2) and not (isinstance(b, int) and (b <= EARLY + 2 or b == NB)):
                            weigh(b - 2, u, (k - 2) % 4)
                        for c in range(IC):
                            if late(b, EARLY + 1):
                                res_gelu(act, b, u, c)
                            if c == 1 and isinstance(b, int) and b == EARLY + 2:
                                weigh(1, 1, 1)
                            if c == 1 and isinstance(b, int) and b == NB - 1:
                                weigh(NB - 2, 1 - u, (k - 1) % 4)
                        if late(b + 2):
                            res_high(act, b + 2, u)
                        if real(b):
                            coefs(b, k)
                        if isinstance(b, int) and b == EARLY + 1:
                            weigh(0, 0, 0)
                        if isinstance(b, int) and b == EARLY + 2:
                            weigh(2, 0, 2)

                    schedule(act, step)

                @block.gpsimd
                def _(po):
                    def index(b, k):
                        wait(po, gathered[k], (b // 4) * 16 * J)
                        po.tensor_copy(idx[:, k:k + 1], slot_all[:, bass.ds(b, 1)]).then_inc(idx_ready, 1)

                    def gather(b, k):
                        for j in range(J):
                            po.indirect_dma_start(out=moe[:, k, j], out_offset=None, in_=moe_dram,
                                                  in_offset=bass.IndirectOffsetOnAxis(ap=idx[:, k, j:j + 1], axis=0),
                                                  bounds_check=S, oob_is_err=False).then_inc(gathered[k], 16)

                    def factor(b, u):
                        po.wait_ge(ve2_ready, b + 1)
                        wait(po, res_ready, J * (b - 1))
                        po.tensor_tensor(rs2[:, u], ve2[:, u], expo[:, 0:J], ALU.pow).then_inc(rs2_ready, 1)

                    for b in range(4):
                        index(b, b)
                    po.wait_ge(idx_ready, 4)
                    for k in range(2):
                        po.wait_ge(e_stored[k], 16 * NT // 2)
                    for b in range(EARLY + 1):
                        gather(b, b)

                    def step(b, u, k):
                        if real(b + 1) and not (isinstance(b, int) and b + 1 < 4):
                            index(b + 1, (k + 1) % 4)
                            po.wait_ge(idx_ready, b + 2)
                            po.wait_ge(y0_ready, J * (b - 2))
                        if real(b - 3):
                            factor(b - 3, 1 - u)
                        if real(b + 1):
                            gather(b + 1, (k + 1) % 4)

                    schedule(po, step)

                @block.vector
                def _(ve):
                    def total(b, u, k):
                        if isinstance(b, int) and b < EARLY:
                            r = r_early[:, b]
                        else:
                            r = psum[4 + k]
                            ve.wait_ge(out2_done, b + 1)
                        ve.wait_ge(y0_ready, J * (b + 1))
                        ve.wait_ge(coef_ready, 2 * b + 2)
                        wait(ve, y2_ready, J * b)
                        for j in range(J):
                            ve.scalar_tensor_tensor(y1[:, j], r[:, j * D:(j + 1) * D], coef[:, k, j, 0:1],
                                                    y0[:, u, j], ALU.mult, ALU.add).then_inc(y1_ready, 1)
                        wait(ve, res_ready, J * (b - 1))
                        for j in range(J):
                            ve.wait_ge(y1_ready, J * b + j + 1)
                            ve.scalar_tensor_tensor(y2[:, u, j], kept[:, bass.ds(b, 1), 0, j * D:(j + 1) * D],
                                                    coef[:, k, j, 3:4], y1[:, j],
                                                    ALU.mult, ALU.add).then_inc(y2_ready, 1)
                        wait(ve, mean2_ready, b)
                        for j in range(J):
                            ve.wait_ge(y2_ready, J * b + j + 1)
                            ve.bn_stats(st2[:, j], y2[:, u, j]).then_inc(st2_ready, 1)
                        ve.wait_ge(st2_ready, J * (b + 1))
                        moments(ve, st2, mom2, var2, mom2_step, MS * b)
                        ve.tensor_scalar(mean2[:, u], mom2[:, :, 0], 0.5, None, ALU.mult).then_inc(mean2_ready, 1)
                        ve.wait_ge(mom2_step, MS * b + MS)
                        wait(ve, rs2_ready, b - 1)
                        ve.tensor_scalar(ve2[:, u], var2[:], LN_EPS, None, ALU.add).then_inc(ve2_ready, 1)

                    def norm(b, u):
                        ve.wait_ge(mean2_ready, b + 1)
                        ve.wait_ge(rs2_ready, b + 1)
                        wait(ve, stored[u], (b // 2) * 16)
                        for j in range(J):
                            ve.tensor_scalar(res[:, u, j], y2[:, u, j], mean2[:, u, j:j + 1], rs2[:, u, j:j + 1],
                                             ALU.subtract, ALU.mult).then_inc(res_ready, 1)

                    def step(b, u, k):
                        first = isinstance(b, int) and b <= EARLY + 2
                        if isinstance(b, int) and b == NB:
                            norm(b - 3, 1 - u)
                        if late(b + 2) and first:
                            res_low(ve, b + 2, u)
                        if real(b - 2):
                            total(b - 2, u, (k - 2) % 4)
                        if late(b + 2) and not first:
                            res_low(ve, b + 2, u)
                        if real(b - 3) and not (isinstance(b, int) and b == NB):
                            norm(b - 3, 1 - u)

                    schedule(ve, step)

                @block.sync
                def _(sp):
                    def step(b, u, k):
                        if real(b - 3):
                            sp.wait_ge(res_ready, J * (b - 2))
                            sp.dma_start(out_v[:, bass.ds(b - 3, 1)], res[:, 1 - u].rearrange("p j d -> p (j d)"))\
                                .then_inc(stored[1 - u], 16)

                    schedule(sp, step)
                    for k in range(2):
                        sp.wait_ge(stored[k], 16 * NB // 2)


_OUT = (16, 512, 128)


def kernel(**inputs):
    import numpy as np
    import concourse.bacc as bacc
    from concourse.bass_utils import run_bass_kernel_spmd

    a = {k.removeprefix("L0_"): np.asarray(v) for k, v in inputs.items()}
    x = a["attn_x"]
    NB, T, D = x.shape
    P_, J = 128, T // 128
    E, _, I = a["ffn_inter_w"].shape
    w = a["attn_w_qkv"]
    c = np.ascontiguousarray
    consts = np.zeros((P_, 2 * P_ + J * E), np.float32)
    consts[:, :P_] = np.eye(P_)
    consts[:, P_:2 * P_] = np.triu(np.ones((P_, P_)), 1)
    consts[:, 2 * P_:] = np.tile(E - np.arange(E), J)
    arrays = {
        "x_tok": c(x),
        "x_T": c(x.reshape(NB, P_, J, D).transpose(3, 0, 2, 1).reshape(D, NB * T)),
        "w_attn": c(np.concatenate([w[:, :D].T, w[:, D:2 * D].T, w[:, 2 * D:].T, a["attn_w_proj"]], axis=1)),
        "b_proj": c(a["attn_b_proj"]),
        "small": c(np.concatenate([
            a["attn_b_qkv"][:D, None], a["attn_b_qkv"][2 * D:, None], a["ffn_attn_nw"][:, None],
            a["ffn_attn_nb"][:, None], a["ffn_wg"], a["ffn_res_coef"], a["ffn_res_inter_b"].reshape(I // P_, P_).T,
            a["ffn_inter_b"].reshape(E * (I // P_), P_).T,
            a["ffn_output_b"].T], axis=1)),
        "inter_w": c(a["ffn_inter_w"]), "output_w": c(a["ffn_output_w"]),
        "res_w": c(a["ffn_res_inter_w"]), "res_out_w": c(a["ffn_res_output_w"]),
        "res_out_b": c(np.tile(a["ffn_res_output_b"], (2, 1))),
        "consts": consts,
    }
    nc = bacc.Bacc("TRN2", target_bir_lowering=False, num_devices=1)
    args = {n: nc.dram_tensor(n, v.shape, mybir.dt.from_np(v.dtype), kind="ExternalInput").ap()
            for n, v in arrays.items()}
    out = nc.dram_tensor("out", _OUT, F32, kind="ExternalOutput").ap()
    build(nc, *args.values(), out)
    r = run_bass_kernel_spmd(nc, [arrays], core_ids=[0])
    return r.results[0]["out"]
```
